# Optimizing a Trainium2 kernel written in Bass

```python
import numpy as np
import jax
import jax.numpy as jnp

def _softmax(x, axis=-1):
    return jax.nn.softmax(x, axis=axis)

def _gelu(x):
    return jax.nn.gelu(x, approximate=True)

def _silu(x):
    return jax.nn.silu(x)

def _sigmoid(x):
    return jax.nn.sigmoid(x)

def _layernorm(x, axis=-1, eps=1e-05):
    m = jnp.mean(x, axis=axis, keepdims=True)
    v = jnp.var(x, axis=axis, keepdims=True)
    return (x - m) / jnp.sqrt(v + eps)

def _scatter_add(tgt, idx, src, axis=0):
    return tgt.at[idx].add(src)

def _segment_sum(src, seg, n):
    return jax.ops.segment_sum(src, seg, n)
kernel_name = 'mk_decoder_preln_d1_seqx_r4_1f12a7'

def setup_inputs(seed: int=0):
    np.random.seed(seed)
    _w = jnp.asarray

    def _rec_inputs():
        import jax
        import jax.numpy as jnp
        _rk = jax.random.key(seed)
        x = 7.22e-05 + 1 * jax.random.normal(jax.random.fold_in(_rk, 1), (4, 1024, 256), jnp.float32)
        _lenS = 1024 - jax.random.randint(jax.random.fold_in(_rk, 7), (4,), 0, max(1, 1024 // 4) + 1, jnp.int32)
        _lenS2 = 77 - jax.random.randint(jax.random.fold_in(_rk, 8), (4,), 0, max(1, 77 // 4) + 1, jnp.int32)
        _ctx_1024P = jax.random.normal(jax.random.fold_in(_rk, 11), (4, 16, 256), jnp.float32)
        _ctx_1024c = jax.random.dirichlet(jax.random.fold_in(_rk, 511), 0.3 * jnp.ones((16,), jnp.float32), (4, 77))
        _ctx_1024t = jnp.einsum('bsk,bkd->bsd', _ctx_1024c, _ctx_1024P)
        _ctx_1024t = _ctx_1024t * jax.lax.rsqrt(jnp.mean(jnp.square(_ctx_1024t)) + 1e-12) * 0.953939
        ctx_1024 = 4.13588e-05 + 0.999923 * (_ctx_1024t + 0.3 * jax.random.normal(jax.random.fold_in(_rk, 611), (4, 77, 256), jnp.float32))
        itok_BxS_1_4095 = jax.random.randint(jax.random.fold_in(_rk, 12), (4, 1024), 1, 1024, jnp.int32)
        return (x, ctx_1024, itok_BxS_1_4095)
    x, ctx_1024, itok_BxS_1_4095 = _rec_inputs()

    def _L0_attn_setup():
        import jax, jax.numpy as jnp
        import numpy as np
        B, L, DM, ED, N, R, K = (2, 256, 256, 512, 16, 64, 4)
        key = jax.random.key(seed)
        ks = jax.random.split(key, 8)
        s = 0.02
        x = jax.random.normal(ks[0], (B, L, DM), jnp.float32)
        in_proj_w = jax.random.normal(ks[1], (2 * ED, DM), jnp.float32) * s
        conv_w = jax.random.normal(ks[2], (ED, 1, K), jnp.float32) * 0.3
        x_proj_w = jax.random.normal(ks[3], (R + 2 * N, ED), jnp.float32) * s
        dt_proj_w = jax.random.normal(ks[4], (ED, R), jnp.float32) * R ** (-0.5)
        dt_proj_b = jax.random.uniform(ks[5], (ED,), jnp.float32, minval=-4.6, maxval=-2.3)
        A_log = jnp.log(jnp.tile(jnp.arange(1, N + 1, dtype=jnp.float32), (ED, 1)))
        D = jnp.ones((ED,), jnp.float32)
        out_proj_w = jax.random.normal(ks[6], (DM, ED), jnp.float32) * s
        return dict(x=x, in_proj_w=in_proj_w, conv_w=conv_w, x_proj_w=x_proj_w, dt_proj_w=dt_proj_w, dt_proj_b=dt_proj_b, A_log=A_log, D=D, out_proj_w=out_proj_w)
    _L0_attn_all = _L0_attn_setup()
    _L0_attn_in = {k: v for k, v in _L0_attn_all.items() if k in ('in_proj_w', 'conv_w', 'x_proj_w', 'dt_proj_w', 'dt_proj_b', 'A_log', 'D', 'out_proj_w')}
    del _L0_attn_all

    def _L0_xattn_setup():
        import jax, jax.numpy as jnp
        import numpy as np
        EMBED_DIM = 256
        NUM_HEADS = 16
        HEAD_DIM = EMBED_DIM // NUM_HEADS
        ROPE_BASE = 10000.0

        def _apply_rope(q, position_ids):
            hd = q.shape[-1]
            inv_freq = 1.0 / ROPE_BASE ** (jnp.arange(0, hd, 2, dtype=jnp.float32) / hd)
            ang = position_ids.astype(jnp.float32)[:, :, None] * inv_freq
            cos = jnp.cos(ang)[:, :, None, :]
            sin = jnp.sin(ang)[:, :, None, :]
            q1, q2 = (q[..., :hd // 2], q[..., hd // 2:])
            return jnp.concatenate([q1 * cos - q2 * sin, q2 * cos + q1 * sin], axis=-1)
        key = jax.random.key(seed)
        ks = jax.random.split(key, 12)
        B, T, M, D = (4, 512, 512, EMBED_DIM)
        query = jax.random.normal(ks[0], (B, T, D), dtype=jnp.float32)
        k_in = jax.random.normal(ks[1], (B, M, D), dtype=jnp.float32)
        v_in = jax.random.normal(ks[2], (B, M, D), dtype=jnp.float32)
        query_position_ids = jnp.sort(jax.random.randint(ks[3], (B, T), 0, 1024), axis=-1).astype(jnp.int64)
        lim = float(np.sqrt(6.0 / (D + D)))
        Wq = jax.random.uniform(ks[4], (D, D), minval=-lim, maxval=lim, dtype=jnp.float32)
        Wk = jax.random.uniform(ks[5], (D, D), minval=-lim, maxval=lim, dtype=jnp.float32)
        Wv = jax.random.uniform(ks[6], (D, D), minval=-lim, maxval=lim, dtype=jnp.float32)
        Wo = jax.random.uniform(ks[7], (D, D), minval=-lim, maxval=lim, dtype=jnp.float32)
        bq = jnp.zeros((D,), jnp.float32)
        bk = jnp.zeros((D,), jnp.float32)
        bv = jnp.zeros((D,), jnp.float32)
        bo = jnp.zeros((D,), jnp.float32)
        return dict(query=query, key=k_in, value=v_in, query_position_ids=query_position_ids, Wq=Wq, bq=bq, Wk=Wk, bk=bk, Wv=Wv, bv=bv, Wo=Wo, bo=bo)
    _L0_xattn_all = _L0_xattn_setup()
    _L0_xattn_in = {k: v for k, v in _L0_xattn_all.items() if k in ('Wq', 'bq', 'Wk', 'bk', 'Wv', 'bv', 'Wo', 'bo')}
    del _L0_xattn_all

    def _L0_ffn_setup():
        import jax, jax.numpy as jnp
        import numpy as np
        H = 256
        F = 1024
        E = 8
        TOP_K = 2
        B, S = (1, 512)
        key = jax.random.key(seed)
        k0, k1, k2, k3 = jax.random.split(key, 4)
        hidden_states = jax.random.normal(k0, (B, S, H), dtype=jnp.float32)
        gate_w = jax.random.normal(k1, (E, H), dtype=jnp.float32) * 0.02
        gate_up_w = jax.random.normal(k2, (E, 2 * F, H), dtype=jnp.float32) * 0.02
        down_w = jax.random.normal(k3, (E, H, F), dtype=jnp.float32) * 0.02
        return {'hidden_states': hidden_states, 'gate_w': gate_w, 'gate_up_w': gate_up_w, 'down_w': down_w}
    _L0_ffn_all = _L0_ffn_setup()
    _L0_ffn_in = {k: v for k, v in _L0_ffn_all.items() if k in ('gate_w', 'gate_up_w', 'down_w')}
    del _L0_ffn_all
    return {'x': x, 'ctx_1024': ctx_1024, 'itok_BxS_1_4095': itok_BxS_1_4095, 'L0_attn_in_proj_w': _L0_attn_in['in_proj_w'], 'L0_attn_conv_w': _L0_attn_in['conv_w'], 'L0_attn_x_proj_w': _L0_attn_in['x_proj_w'], 'L0_attn_dt_proj_w': _L0_attn_in['dt_proj_w'], 'L0_attn_dt_proj_b': _L0_attn_in['dt_proj_b'], 'L0_attn_A_log': _L0_attn_in['A_log'], 'L0_attn_D': _L0_attn_in['D'], 'L0_attn_out_proj_w': _L0_attn_in['out_proj_w'], 'L0_xattn_Wq': _L0_xattn_in['Wq'], 'L0_xattn_bq': _L0_xattn_in['bq'], 'L0_xattn_Wk': _L0_xattn_in['Wk'], 'L0_xattn_bk': _L0_xattn_in['bk'], 'L0_xattn_Wv': _L0_xattn_in['Wv'], 'L0_xattn_bv': _L0_xattn_in['bv'], 'L0_xattn_Wo': _L0_xattn_in['Wo'], 'L0_xattn_bo': _L0_xattn_in['bo'], 'L0_ffn_gate_w': _L0_ffn_in['gate_w'], 'L0_ffn_gate_up_w': _L0_ffn_in['gate_up_w'], 'L0_ffn_down_w': _L0_ffn_in['down_w']}

def reference(x, ctx_1024, itok_BxS_1_4095, L0_attn_in_proj_w, L0_attn_conv_w, L0_attn_x_proj_w, L0_attn_dt_proj_w, L0_attn_dt_proj_b, L0_attn_A_log, L0_attn_D, L0_attn_out_proj_w, L0_xattn_Wq, L0_xattn_bq, L0_xattn_Wk, L0_xattn_bk, L0_xattn_Wv, L0_xattn_bv, L0_xattn_Wo, L0_xattn_bo, L0_ffn_gate_w, L0_ffn_gate_up_w, L0_ffn_down_w):
    import jax
    import jax.numpy as jnp

    def _L0_attn_ref(x, in_proj_w, conv_w, x_proj_w, dt_proj_w, dt_proj_b, A_log, D, out_proj_w):
        import jax, jax.numpy as jnp
        import numpy as np
        B, L, DM, ED, N, R, K = (2, 256, 256, 512, 16, 64, 4)
        xz = jnp.einsum('bld,ed->ble', x, in_proj_w)
        xp, z = (xz[..., :ED], xz[..., ED:])
        xc = jax.lax.conv_general_dilated(xp.transpose(0, 2, 1), conv_w, window_strides=(1,), padding=[(K - 1, 0)], feature_group_count=ED, dimension_numbers=('NCH', 'OIH', 'NCH'))
        xc = jax.nn.silu(xc.transpose(0, 2, 1))
        dBC = jnp.einsum('ble,fe->blf', xc, x_proj_w)
        dt, Bm, Cm = (dBC[..., :R], dBC[..., R:R + N], dBC[..., R + N:])
        delta = jax.nn.softplus(jnp.einsum('blr,er->ble', dt, dt_proj_w) + dt_proj_b)
        A = -jnp.exp(A_log)
        dA = jnp.exp(delta[..., None] * A)
        BX = delta[..., None] * Bm[:, :, None, :] * xc[..., None]

        def comb(c1, c2):
            a1, b1 = c1
            a2, b2 = c2
            return (a1 * a2, b1 * a2 + b2)
        _, hs = jax.lax.associative_scan(comb, (dA, BX), axis=1)
        y = jnp.einsum('blen,bln->ble', hs, Cm) + D * xc
        out = jnp.einsum('ble,de->bld', y * jax.nn.silu(z), out_proj_w)
        return out

    def _L0_xattn_ref(query, key, value, query_position_ids, Wq, bq, Wk, bk, Wv, bv, Wo, bo):
        import jax, jax.numpy as jnp
        import numpy as np
        EMBED_DIM = 256
        NUM_HEADS = 16
        HEAD_DIM = EMBED_DIM // NUM_HEADS
        ROPE_BASE = 10000.0

        def _apply_rope(q, position_ids):
            hd = q.shape[-1]
            inv_freq = 1.0 / ROPE_BASE ** (jnp.arange(0, hd, 2, dtype=jnp.float32) / hd)
            ang = position_ids.astype(jnp.float32)[:, :, None] * inv_freq
            cos = jnp.cos(ang)[:, :, None, :]
            sin = jnp.sin(ang)[:, :, None, :]
            q1, q2 = (q[..., :hd // 2], q[..., hd // 2:])
            return jnp.concatenate([q1 * cos - q2 * sin, q2 * cos + q1 * sin], axis=-1)
        B, T, D = query.shape
        M = key.shape[1]
        H, hd = (NUM_HEADS, HEAD_DIM)
        scaling = 1.0 / np.sqrt(hd)
        q = (query @ Wq.T + bq).reshape(B, T, H, hd)
        k = (key @ Wk.T + bk).reshape(B, M, H, hd)
        v = (value @ Wv.T + bv).reshape(B, M, H, hd)
        q = _apply_rope(q, query_position_ids)
        scores = jnp.einsum('bthd,bmhd->bhtm', q, k) * scaling
        attn = jax.nn.softmax(scores, axis=-1)
        out = jnp.einsum('bhtm,bmhd->bthd', attn, v).reshape(B, T, D)
        return out @ Wo.T + bo

    def _L0_ffn_ref(hidden_states, gate_w, gate_up_w, down_w):
        import jax, jax.numpy as jnp
        import numpy as np
        H = 256
        F = 1024
        E = 8
        TOP_K = 2
        B, S = (1, 512)
        b, s, h = hidden_states.shape
        x = hidden_states.reshape(-1, h)
        router_logits = x @ gate_w.T
        probs = jax.nn.softmax(router_logits.astype(jnp.float32), axis=-1)
        topw, sel = jax.lax.top_k(probs, TOP_K)
        topw = topw / jnp.sum(topw, axis=-1, keepdims=True)
        topw = topw.astype(x.dtype)
        combine = jnp.sum(jax.nn.one_hot(sel, E, dtype=x.dtype) * topw[..., None], axis=1)
        gu = jnp.einsum('th,efh->etf', x, gate_up_w)
        gate, up = (gu[..., :F], gu[..., F:])
        hact = up * jax.nn.gelu(gate, approximate=False)
        expert_out = jnp.einsum('etf,ehf->eth', hact, down_w)
        out = jnp.einsum('eth,te->th', expert_out, combine)
        return out.reshape(b, s, h)
    x = x + _L0_attn_ref(_layernorm(x, axis=-1), L0_attn_in_proj_w, L0_attn_conv_w, L0_attn_x_proj_w, L0_attn_dt_proj_w, L0_attn_dt_proj_b, L0_attn_A_log, L0_attn_D, L0_attn_out_proj_w)
    x = x + _L0_xattn_ref(_layernorm(x, axis=-1), ctx_1024, ctx_1024, itok_BxS_1_4095, L0_xattn_Wq, L0_xattn_bq, L0_xattn_Wk, L0_xattn_bk, L0_xattn_Wv, L0_xattn_bv, L0_xattn_Wo, L0_xattn_bo)
    x = x + _L0_ffn_ref(_layernorm(x, axis=-1), L0_ffn_gate_w, L0_ffn_gate_up_w, L0_ffn_down_w)
    return x

_drawn_inputs = setup_inputs


def setup_inputs(seed=0):
    import zlib

    import numpy as np

    out = dict(_drawn_inputs(seed))
    spreads = {'L0_attn_D': (1.0, 0.2),
     'L0_xattn_bq': (0.0, 0.1),
     'L0_xattn_bk': (0.0, 0.1),
     'L0_xattn_bv': (0.0, 0.1),
     'L0_xattn_bo': (0.0, 0.1)}
    factors = {}
    for name, (base, spread) in spreads.items():
        noise = np.random.default_rng([zlib.crc32(name.encode()), seed]).standard_normal(out[name].shape)
        drawn = base * np.exp(spread * noise) if base else spread * noise
        out[name] = jnp.asarray(drawn.astype(out[name].dtype))
    for name, factor in factors.items():
        out[name] = (out[name] * factor).astype(out[name].dtype)
    return out
```

```python
import numpy as np
import concourse.bass as bass
from concourse import mybir
from contextlib import ExitStack

F32, BF16, I32, U32 = mybir.dt.float32, mybir.dt.bfloat16, mybir.dt.int32, mybir.dt.uint32
ACT = mybir.ActivationFunctionType
ALU = mybir.AluOpType
AXX = mybir.AxisListType.X
P = 128
BANK = 512
EPS = 1e-5

PAD = 8
SLOTS = 4
LOADS = 48

def mamba_phase(nc, x, in_w, conv_w, xproj_w, dtproj_w, dtproj_b, a_log, d_vec, out_w, ident_c, sel_c, c_rows_dram, x1):
    NB, T, DM = x.shape
    ED, KC = conv_w.shape
    N = a_log.shape[1]
    R = dtproj_w.shape[0]
    KD = DM // P
    KE = ED // P
    NT = T // P
    H = T // BANK
    LAG = 3

    with ExitStack() as ctx:
        def sb(name, shape, dt=F32):
            return ctx.enter_context(nc.sbuf_tensor(name, shape, dt))

        def sem(name):
            return ctx.enter_context(nc.semaphore(name))

        ident = sb("m_ident", [P, P])
        w_in = sb("m_w_in", [P, KD, 2 * ED])
        w_xdt = sb("m_w_xdt", [P, KE, 96])
        w_xb = sb("m_w_xb", [P, KE, 96])
        w_dt = sb("m_w_dt", [R, ED])
        w_out = sb("m_w_out", [P, KE, DM])
        wconv = sb("m_wconv", [P, KE, KC])
        b_dt = sb("m_b_dt", [P, KE])
        negA = sb("m_negA", [P, KE, N])
        dvec = sb("m_dvec", [P, KE])
        sel = sb("m_sel", [96, N, P], BF16)
        x_sb = sb("m_x", [P, NT, DM])
        stats = sb("m_stats", [P, NT, 6])
        mv = sb("m_mv", [P, NT, 2])
        rstd = sb("m_rstd", [P, NT])
        silu_z = sb("m_silu_z", [P, KE, T])
        xc = sb("m_xc", [P, KE, T])
        delta = sb("m_delta", [P, KE, T])
        u = sb("m_u", [P, KE, T])
        c_bc = sb("m_c_bc", [P, N, T])
        b_split = sb("m_b_split", [96, T], BF16)
        y_sum = sb("m_y_sum", [P, T])
        AH, HC = 2, 4
        region = sb("m_region", [P, 8 * T + 64])
        a_ring = [region[:, i * T:(i + 1) * T] for i in range(AH)]
        h_ring = [region[:, (AH + i) * T:(AH + i + 1) * T] for i in range(AH)]
        hc_ring = [region[:, (2 * AH + i) * T:(2 * AH + i + 1) * T] for i in range(HC)]
        XPW = T + KC - 1
        xp = region[:, 0:KE * XPW].rearrange("p (c t) -> p c t", c=KE)
        q0 = KE * XPW + 4
        xnT = region[:, q0:q0 + KD * T].rearrange("p (c t) -> p c t", c=KD)
        q1 = q0 + KD * T
        xn = region[:, q1:q1 + NT * DM].rearrange("p (i d) -> p i d", i=NT)
        dt_rows = region[:, q0:q0 + T]
        b_rows = region[0:96, q0 + T:q0 + 2 * T]
        b_res = region[0:96, q1:q1 + T]
        b_part = region[0:96, q1 + T:q1 + T + T // 2].bitcast(BF16)
        ps = ctx.enter_context(nc.psum_tensor("m_ps", [P, 8, BANK], F32))
        sel_stage = silu_z[0:96, 0:2, :].rearrange("p a (n m) -> p (a n) m", m=P)

        consts = sem("m_consts")
        pads = sem("m_pads")
        sel_ready = sem("m_sel_ready")
        negA_ready = sem("m_negA_ready")
        x_loaded = sem("m_x_loaded")
        dve_ln = sem("m_dve_ln")
        rstd_ready = sem("m_rstd_ready")
        xn_ready = sem("m_xn_ready")
        proj_done = sem("m_proj_done")
        evac_done = sem("m_evac_done")
        conv_step = sem("m_conv_step")
        conv_done = sem("m_conv_done")
        silu_done = sem("m_silu_done")
        pool_b = sem("m_pool_b")
        c_stored = sem("m_c_stored")
        cb_loaded = [sem(f"m_cb_loaded{g}") for g in range(4)]
        neg_abs = sem("m_neg_abs")
        exp1_done = sem("m_exp1_done")
        ln_done = sem("m_ln_done")
        dve_delta = sem("m_dve_delta")
        bcast_done = sem("m_bcast_done")
        a_ready = sem("m_a_ready")
        bx_done = sem("m_bx_done")
        scan_done = sem("m_scan_done")
        hc_done = sem("m_hc_done")
        yacc_done = sem("m_yacc_done")
        y_read = sem("m_y_read")
        gated = sem("m_gated")
        out_done = sem("m_out_done")
        res_done = sem("m_res_done")
        x1_stored = sem("m_x1_stored")
        held = sem("m_held")

        def hold(eng, of, value):
            eng.wait_ge(of, value)
            eng.sem_inc(held, 1)

        G = 4
        J_IN, J_X, J_DT = 4, 4 + 16, 4 + 16 + 4
        JOBS = J_DT + KE * H
        STEPS = KE * N
        LN_STEPS = 2 * NT + 2

        block = ctx.enter_context(nc.Block())

        ONE = 1

        @block.sync
        def _(sp):
            for s in (res_done, y_read, gated, bcast_done, pool_b):
                sp.sem_inc(s, ONE)
            sp.wait_ge(pads, 2)
            for dst, src in [(ident[:], ident_c), (w_in[:], in_w.rearrange("(c p) e -> p c e", p=P)),
                             (w_dt[:], dtproj_w), (w_out[:], out_w.rearrange("(c p) d -> p c d", p=P)),
                             (wconv[:], conv_w.rearrange("(c p) k -> p c k", p=P)),
                             (b_dt[:], dtproj_b),
                             (negA[:], a_log.rearrange("(c p) n -> p c n", p=P)),
                             (dvec[:], d_vec),
                             (sel_stage, sel_c.rearrange("k (n m) -> k n m", m=P))]:
                sp.dma_start(dst, src).then_inc(consts, 16)
            xw = xproj_w.rearrange("(c p) f -> p c f", p=P)
            for dst, lo, hi in [(w_xdt[:, :, 0:R], 0, R), (w_xdt[:, :, R:R + N], R + N, R + 2 * N),
                                (w_xb[:, :, 0:N], R, R + N), (w_xb[:, :, 32:32 + N], R, R + N),
                                (w_xb[:, :, 64:64 + N], R, R + N)]:
                sp.dma_start(dst, xw[:, :, lo:hi]).then_inc(consts, 16)
            with sp.Fori(0, NB) as b:
                sp.wait_ge(res_done, ONE + NT * b)
                sp.dma_start(x_sb[:], x[b].rearrange("(i p) d -> p i d", p=P)).then_inc(x_loaded, 16)
                sp.wait_ge(evac_done, JOBS * b + J_X + H)
                sp.dma_start(c_rows_dram[b], dt_rows[R:R + N, :]).then_inc(c_stored, 16)
                sp.wait_ge(c_stored, 16 * b + 16)
                sp.wait_ge(hc_done, AH + STEPS * b)
                for g in range(G):
                    src = c_rows_dram[b, g * (N // G):(g + 1) * (N // G), :]
                    sp.dma_start(c_bc[:, g * (N // G):(g + 1) * (N // G), :],
                                 src.unsqueeze(0).to_broadcast([P, N // G, T])).then_inc(cb_loaded[g], 16)
                sp.wait_ge(res_done, ONE + NT * b + NT)
                sp.dma_start(x1[b].rearrange("(i p) d -> p i d", p=P), x_sb[:]).then_inc(x1_stored, 16)
                hold(sp, x1_stored, 16 * b + 16)
            sp.wait_ge(x1_stored, 16 * NB)

        @block.gpsimd
        def _(pool):
            nc.gpsimd.memset(w_xdt[:], 0.0).then_inc(pads, 1)
            nc.gpsimd.memset(w_xb[:], 0.0).then_inc(pads, 1)
            pool.wait_ge(consts, 16 * 14)
            nc.gpsimd.tensor_copy(sel[:], sel_stage).then_inc(sel_ready, 1)
            nc.gpsimd.sem_inc(hc_done, AH)
            with pool.Fori(0, NB) as b:
                hold(pool, yacc_done, HC + STEPS * b)
                nc.gpsimd.memset(xp[:, :, 0:KC - 1], 0.0).then_inc(pads, 1)
                pool.wait_ge(evac_done, JOBS * b + J_X + 2 * H)
                pool.wait_ge(bcast_done, ONE + STEPS * b)
                k = 0
                for i in range(3):
                    src = b_rows if i == 0 else b_res
                    hold(pool, pool_b, ONE + 8 * b + k)
                    nc.gpsimd.tensor_copy(b_part, src).then_inc(pool_b, 1)
                    k += 1
                    hold(pool, pool_b, ONE + 8 * b + k)
                    nc.gpsimd.tensor_copy(b_split[32 * i:32 * i + 32, :],
                                          b_part[32 * i:32 * i + 32, :]).then_inc(pool_b, 1)
                    k += 1
                    hold(pool, pool_b, ONE + 8 * b + k)
                    if i < 2:
                        nc.gpsimd.tensor_tensor(b_res, src, b_part, ALU.subtract).then_inc(pool_b, 1)
                        k += 1
                        pool.wait_ge(pool_b, ONE + 8 * b + k)
                assert k == 8
                hold(pool, pool_b, ONE + 8 * b + 8)
                with pool.Fori(0, KE // 2) as pair:
                    ep = 2 * pair
                    for j in range(2 * N):
                        s = b * STEPS + ep * N + j
                        if j < N and j % (N // G) == 0:
                            pool.wait_ge(cb_loaded[j // (N // G)], 16 * b + 16)
                        pool.wait_ge(scan_done, AH + 1 + s)
                        pool.wait_ge(yacc_done, 1 + s)
                        nc.gpsimd.tensor_tensor(hc_ring[j % HC], h_ring[j % AH], c_bc[:, j % N, :],
                                                ALU.mult).then_inc(hc_done, 1)

        @block.scalar
        def _(act):
            act.wait_ge(consts, 16 * 14)
            nc.scalar.activation(negA[:], negA[:], ACT.Exp).then_inc(negA_ready, 1)
            act.wait_ge(negA_ready, 1)
            nc.scalar.activation(negA[:], negA[:], ACT.Copy, scale=-1.0).then_inc(negA_ready, 1)
            act.wait_ge(sel_ready, 1)
            with act.Fori(0, NB) as b:
                def emptied(j, out, func, **kw):
                    act.wait_ge(proj_done, JOBS * b + j + 1)
                    nc.scalar.activation(out, ps[0:out.shape[0], j % 8, :], func, **kw).then_inc(evac_done, 1)

                act.wait_ge(dve_ln, LN_STEPS * b + LN_STEPS)
                nc.scalar.activation(rstd[:], rstd[:], ACT.Sqrt).then_inc(rstd_ready, 1)
                act.wait_ge(yacc_done, HC + STEPS * b)
                j = 0
                for c in range(KD):
                    for h in range(H):
                        emptied(j, xnT[:, c, h * BANK:(h + 1) * BANK], ACT.Copy)
                        j += 1
                act.wait_ge(gated, ONE + KE * b)
                for e in range(2 * KE):
                    for h in range(H):
                        cols = slice(h * BANK, (h + 1) * BANK)
                        if e < KE:
                            emptied(j, xp[:, e, KC - 1 + h * BANK:KC - 1 + (h + 1) * BANK], ACT.Copy)
                        else:
                            emptied(j, silu_z[:, e - KE, cols], ACT.Silu)
                        j += 1
                for e in range(KE):
                    act.wait_ge(conv_done, KE * b + e + 1)
                    nc.scalar.activation(xc[:, e, :], xc[:, e, :], ACT.Silu).then_inc(silu_done, 1)
                for dst, rows in ((dt_rows, 96), (b_rows, 96)):
                    for h in range(H):
                        emptied(j, dst[0:rows, h * BANK:(h + 1) * BANK], ACT.Copy)
                        j += 1
                for e in range(KE):
                    for h in range(H):
                        emptied(j, delta[:, e, h * BANK:(h + 1) * BANK], ACT.Identity, bias=b_dt[:, e:e + 1])
                        j += 1
                for e in range(KE):
                    act.wait_ge(neg_abs, KE * b + e + 1)
                    nc.scalar.activation(u[:, e, :], u[:, e, :], ACT.Exp).then_inc(exp1_done, 1)
                for e in range(KE):
                    act.wait_ge(exp1_done, KE * b + e + 1)
                    nc.scalar.activation(u[:, e, :], u[:, e, :], ACT.Ln, bias=1.0).then_inc(ln_done, 1)
                with act.Fori(0, KE // 2) as pair:
                    ep = 2 * pair
                    for j2 in range(2 * N):
                        s = b * STEPS + ep * N + j2
                        if j2 % N == 0:
                            act.wait_ge(dve_delta, 2 * KE * b + 2 * KE)
                        act.wait_ge(scan_done, 1 + s)
                        e = ep + j2 // N
                        nc.scalar.activation(a_ring[j2 % AH], delta[:, e, :], ACT.Exp,
                                             scale=negA[:, e, j2 % N:j2 % N + 1]).then_inc(a_ready, 1)

        @block.vector
        def _(dve):
            nc.vector.sem_inc(scan_done, AH)
            with dve.Fori(0, NB) as b:
                dve.wait_ge(x_loaded, 16 * b + 16)
                dve.wait_ge(yacc_done, HC + STEPS * b)
                for i in range(NT):
                    nc.vector.bn_stats(stats[:, i, :], x_sb[:, i, :]).then_inc(dve_ln, 1)
                for i in range(NT):
                    hold(dve, dve_ln, LN_STEPS * b + i + 1)
                    nc.vector.bn_aggr(mv[:, i, :], stats[:, i, :]).then_inc(dve_ln, 1)
                dve.wait_ge(dve_ln, LN_STEPS * b + 2 * NT)
                nc.vector.tensor_scalar(rstd[:], mv[:, :, 1], EPS, None, ALU.add).then_inc(dve_ln, 1)
                dve.wait_ge(dve_ln, LN_STEPS * b + 2 * NT + 1)
                nc.vector.reciprocal(rstd[:], rstd[:]).then_inc(dve_ln, 1)
                dve.wait_ge(rstd_ready, b + 1)
                for i in range(NT):
                    nc.vector.tensor_scalar(xn[:, i, :], x_sb[:, i, :], mv[:, i, 0:1], rstd[:, i:i + 1],
                                            ALU.subtract, ALU.mult).then_inc(xn_ready, 1)
                dve.wait_ge(consts, 16 * 14)
                dve.wait_ge(pads, 3 + b)
                for e in range(KE):
                    dve.wait_ge(evac_done, JOBS * b + J_IN + H * (e + 1))
                    nc.vector.tensor_scalar(xc[:, e, :], xp[:, e, 0:T], wconv[:, e, 0:1], None,
                                            ALU.mult).then_inc(conv_step, 1)
                    for k in range(1, KC):
                        dve.wait_ge(conv_step, (KC - 1) * KE * b + (KC - 1) * e + k)
                        nc.vector.scalar_tensor_tensor(
                            out=xc[:, e, :], in0=xp[:, e, k:k + T], scalar=wconv[:, e, k:k + 1], in1=xc[:, e, :],
                            op0=ALU.mult, op1=ALU.add).then_inc(conv_done if k == KC - 1 else conv_step, 1)
                for e in range(KE):
                    dve.wait_ge(evac_done, JOBS * b + J_DT + H * (e + 1))
                    nc.vector.scalar_tensor_tensor(out=u[:, e, :], in0=delta[:, e, :], scalar=-1.0,
                                                   in1=delta[:, e, :], op0=ALU.mult, op1=ALU.min).then_inc(neg_abs, 1)
                for e in range(KE):
                    dve.wait_ge(ln_done, KE * b + e + 1)
                    nc.vector.scalar_tensor_tensor(out=delta[:, e, :], in0=delta[:, e, :], scalar=0.0,
                                                   in1=u[:, e, :], op0=ALU.max, op1=ALU.add).then_inc(dve_delta, 1)
                for e in range(KE):
                    dve.wait_ge(dve_delta, 2 * KE * b + KE + e)
                    dve.wait_ge(silu_done, KE * b + e + 1)
                    nc.vector.tensor_tensor(u[:, e, :], delta[:, e, :], xc[:, e, :],
                                            ALU.mult).then_inc(dve_delta, 1)
                dve.wait_ge(dve_delta, 2 * KE * b + 2 * KE)
                hold(dve, c_stored, 16 * b + 16)
                with dve.Fori(0, KE // 2) as pair:
                    ep = 2 * pair
                    def bx(j2):
                        s = b * STEPS + ep * N + j2
                        dve.wait_ge(bcast_done, ONE + 1 + s)
                        pb = ps[:, 2 * (j2 % 2):2 * (j2 % 2) + 2, :].rearrange("p a t -> p (a t)")
                        nc.vector.tensor_tensor(pb, u[:, ep + j2 // N, :], pb, ALU.mult).then_inc(bx_done, 1)

                    def finish_y(half):
                        e = ep + half
                        dve.wait_ge(yacc_done, HC + b * STEPS + ep * N + (half + 1) * N)
                        yp = ps[:, 4 + 2 * half:6 + 2 * half, :].rearrange("p a t -> p (a t)")
                        nc.vector.scalar_tensor_tensor(out=y_sum[:], in0=xc[:, e, :], scalar=dvec[:, bass.ds(e, 1)], in1=yp,
                                                       op0=ALU.mult, op1=ALU.add).then_inc(y_read, 1)
                        dve.wait_ge(y_read, ONE + b * KE + ep + half + 1)
                        nc.vector.tensor_tensor(u[:, e, :], y_sum[:], silu_z[:, e, :],
                                                ALU.mult).then_inc(gated, 1)
                        dve.wait_ge(gated, ONE + b * KE + ep + half + 1)

                    bx(0)
                    for j2 in range(2 * N):
                        s = b * STEPS + ep * N + j2
                        if j2 + 1 < 2 * N:
                            bx(j2 + 1)
                        dve.wait_ge(bx_done, 1 + s)
                        dve.wait_ge(a_ready, 1 + s)
                        dve.wait_ge(hc_done, 1 + s)
                        pb = ps[:, 2 * (j2 % 2):2 * (j2 % 2) + 2, :].rearrange("p a t -> p (a t)")
                        nc.vector.tensor_tensor_scan(h_ring[j2 % AH], a_ring[j2 % AH], pb, 0.0,
                                                     ALU.mult, ALU.add).then_inc(scan_done, 1)
                        if j2 == N + 5:
                            finish_y(0)
                    finish_y(1)
                for i in range(NT):
                    dve.wait_ge(out_done, NT * b + i + 1)
                    nc.vector.tensor_tensor(x_sb[:, i, :], ps[:, i % 4, 0:DM], x_sb[:, i, :],
                                            ALU.add).then_inc(res_done, 1)

        @block.tensor
        def _(pe):
            pe.wait_ge(consts, 16 * 14)
            pe.wait_ge(sel_ready, 1)
            nc.tensor.sem_inc(yacc_done, HC)
            with pe.Fori(0, NB) as b:
                pe.wait_ge(res_done, ONE + NT * b)
                pe.wait_ge(y_read, ONE + KE * b)
                def bank_free(j):
                    if j >= 8:
                        pe.wait_ge(evac_done, JOBS * b + j - 7)

                j = 0
                for c in range(KD):
                    for h in range(H):
                        for i in range(4):
                            if c == 0:
                                pe.wait_ge(xn_ready, NT * b + 4 * h + i + 1)
                            last = nc.tensor.transpose(ps[:, j % 8, i * P:(i + 1) * P],
                                                       xn[:, 4 * h + i, c * P:(c + 1) * P], ident[:])
                        last.then_inc(proj_done, 1)
                        j += 1
                pe.wait_ge(evac_done, JOBS * b + J_IN)
                for e in range(2 * KE):
                    for h in range(H):
                        bank_free(j)
                        for c in range(KD):
                            last = nc.tensor.matmul(ps[:, j % 8, :], w_in[:, c, e * P:(e + 1) * P],
                                                    xnT[:, c, h * BANK:(h + 1) * BANK],
                                                    start=(c == 0), stop=(c == KD - 1))
                        last.then_inc(proj_done, 1)
                        j += 1
                pe.wait_ge(silu_done, KE * b + KE)
                for w in (w_xdt, w_xb):
                    for h in range(H):
                        bank_free(j)
                        for c in range(KE):
                            last = nc.tensor.matmul(ps[0:96, j % 8, :], w[:, c, :], xc[:, c, h * BANK:(h + 1) * BANK],
                                                    start=(c == 0), stop=(c == KE - 1))
                        last.then_inc(proj_done, 1)
                        j += 1
                pe.wait_ge(evac_done, JOBS * b + J_X + H)
                for e in range(KE):
                    for h in range(H):
                        bank_free(j)
                        nc.tensor.matmul(ps[:, j % 8, :], w_dt[:, e * P:(e + 1) * P],
                                         dt_rows[0:R, h * BANK:(h + 1) * BANK],
                                         start=True, stop=True).then_inc(proj_done, 1)
                        j += 1
                pe.wait_ge(evac_done, JOBS * b + JOBS)
                hold(pe, pool_b, ONE + 8 * b + 8)
                with pe.Fori(0, KE // 2) as pair:
                    ep = 2 * pair
                    def bcast(j2):
                        s = b * STEPS + ep * N + j2
                        pe.wait_ge(scan_done, 1 + s)
                        for h in range(H):
                            last = nc.tensor.matmul(ps[:, 2 * (j2 % 2) + h, :], sel[:, j2 % N, :],
                                                    b_split[:, h * BANK:(h + 1) * BANK], start=True, stop=True)
                        last.then_inc(bcast_done, 1)

                    def yacc(j2):
                        s = b * STEPS + ep * N + j2
                        n, half = j2 % N, j2 // N
                        pe.wait_ge(hc_done, AH + 1 + s)
                        if n == 0:
                            pe.wait_ge(y_read, ONE + b * KE + ep + max(0, half - 1))
                        for h in range(H):
                            last = nc.tensor.matmul(ps[:, 4 + 2 * half + h, :], ident[:],
                                                    hc_ring[j2 % HC][:, h * BANK:(h + 1) * BANK],
                                                    start=(n == 0), stop=(n == N - 1))
                        last.then_inc(yacc_done, 1)

                    for j2 in range(2 * N + LAG):
                        if j2 < 2 * N:
                            bcast(j2)
                        if j2 >= LAG:
                            yacc(j2 - LAG)
                pe.wait_ge(gated, ONE + KE * b + KE)
                for i in range(NT):
                    if i >= 4:
                        pe.wait_ge(res_done, ONE + NT * b + i - 3)
                    for c in range(KE):
                        last = nc.tensor.matmul(ps[:, i % 4, 0:DM], u[:, c, i * P:(i + 1) * P], w_out[:, c, :],
                                                start=(c == 0), stop=(c == KE - 1))
                    last.then_inc(out_done, 1)


def attention_phase(nc, x1, ctx_t, pos, wq, wk, wv, wo, bq, bk, bv, bo, ident_c, head_mask_c, inv_freq_c, gate_w,
                    x2, xrow, logits):
    NBR, T, DM = x1.shape
    M = ctx_t.shape[1] // NBR
    NH, HD, E = 16, 16, gate_w.shape[1]
    HP = NH // 2
    KD = DM // P
    CH = BANK
    TI = CH // P
    NC = NBR * T // CH
    CB = T // CH
    HM = HP // 2 * M
    SCALE = HD ** -0.5
    TWO_PI = 2 * np.pi
    C1 = 6.28125
    C2 = float(np.float32(np.floor((TWO_PI - C1) * 2 ** 20) / 2 ** 20))
    C3 = TWO_PI - C1 - C2
    ROUND = 1.5 * 2 ** 23
    PI_IN = 3.1415925

    x1c = x1.rearrange("b (c i p) d -> (b c) p i d", p=P, i=TI)
    x2c = x2.rearrange("b (c i p) d -> (b c) p i d", p=P, i=TI)

    with ExitStack() as ctx:
        def sb(name, shape, dt=F32):
            return ctx.enter_context(nc.sbuf_tensor(name, shape, dt))

        def sem(name):
            return ctx.enter_context(nc.semaphore(name))

        ident = sb("t_ident", [P, P])
        wq_sb, wk_sb, wv_sb, wo_sb = (sb(f"t_{n}", [P, KD, DM]) for n in ("wq", "wk", "wv", "wo"))
        gw_sb = sb("t_gw", [P, KD, E])
        bq_bc, bv_bc, bo_bc = (sb(f"t_{n}", [P, DM]) for n in ("bq", "bv", "bo"))
        bk_col = sb("t_bk", [P, KD])
        mask = sb("t_mask", [P, HP])
        inv_freq = sb("t_inv_freq", [P, HD // 2])
        k_blk = sb("t_k_blk", [P, KD, NBR, HP * M])
        v_pad = sb("t_v_pad", [M, NBR, NH, 2 * HD])
        v_cur = sb("t_v_cur", [M, NH, 2 * HD])
        pos_i = sb("t_pos_i", [P, NC * TI], I32)
        pos_f = sb("t_pos_f", [P, NC * TI])
        trig = [sb(f"t_trig{i}", [P, NC * TI, HD // 2]) for i in range(5)]
        ang, turns, sin_t, cos_t, tmp_t = trig
        xa = sb("t_xa", [P, NC, TI, DM])
        stats = sb("t_stats", [P, TI, 6])
        mv1, mv2 = sb("t_mv1", [P, TI, 2]), sb("t_mv2", [P, TI, 2])
        rstd1, rstd2 = sb("t_rstd1", [P, TI]), sb("t_rstd2", [P, TI])
        stats2 = sb("t_stats2", [P, TI, 6])
        xn = sb("t_xn", [P, TI, DM])
        xnT = sb("t_xnT", [P, KD, CH])
        q = sb("t_q", [P, TI, DM])
        q_rot = sb("t_q_rot", [P, TI, DM])
        rope_a = sb("t_rope_a", [P, TI, NH, HD // 2])
        rope_b = sb("t_rope_b", [P, TI, NH, HD // 2])
        qT = sb("t_qT", [P, 2, KD, CH])
        probs = sb("t_probs", [P, 2, TI, NH * M])
        early = probs[:, 0, :, :].rearrange("p i (c n) -> p i c n", c=2)
        ctxT, kT = early[:, 0, :, 0:NBR * M], early[:, 1, :, 0:NBR * M]
        mx = sb("t_mx", [P, 2, HP])
        total = sb("t_total", [P, 2, HP])
        rtotal = sb("t_rtotal", [P, 4, HP])
        pT = sb("t_pT", [M, 4, CH])
        oT = sb("t_oT", [P, 2, KD, CH])
        xn2s = sb("t_xn2s", [P, TI, DM])
        xn2T = sb("t_xn2T", [P, KD, CH])
        ps = ctx.enter_context(nc.psum_tensor("t_ps", [P, 8, BANK], F32))
        S_BANK, T_BANK, O_BANK, JOB_BANK = 0, 4, 6, 7

        consts = sem("t_consts")
        held = sem("t_held")
        v_zeroed = sem("t_v_zeroed")
        k_done, k_evac, k_blocks = sem("t_k_done"), sem("t_k_evac"), sem("t_k_blocks")
        v_done, v_evac, v_copied = sem("t_v_done"), sem("t_v_evac"), sem("t_v_copied")
        trig_step, sin_done = sem("t_trig_step"), sem("t_sin_done")
        x_loaded = sem("t_x_loaded")
        ln1, rstd1_ready, xn_ready = sem("t_ln1"), sem("t_rstd1_ready"), sem("t_xn_ready")
        a_job, a_evac = sem("t_a_job"), sem("t_a_evac")
        d_job, d_evac = sem("t_d_job"), sem("t_d_evac")
        rope_step = sem("t_rope_step")
        s_done, mx_done, sub_done, exp_done = sem("t_s_done"), sem("t_mx_done"), sem("t_sub_done"), sem("t_exp_done")
        sum_done, rs_done, norm_done = sem("t_sum_done"), sem("t_rs_done"), sem("t_norm_done")
        tr_done, tr_evac, pv_done, o_evac = sem("t_tr_done"), sem("t_tr_evac"), sem("t_pv_done"), sem("t_o_evac")
        bo_added = sem("t_bo_added")
        ln2, rstd2_ready, xn2_ready = sem("t_ln2"), sem("t_rstd2_ready"), sem("t_xn2_ready")
        x2_stored, xn2_kept = sem("t_x2_stored"), sem("t_xn2_kept")
        N_CONST = 16 * 15
        AJ, DJ, HT = 6, 5, 2 * TI
        LN = 2 * TI + 2

        def hold(eng, of, value):
            eng.wait_ge(of, value)
            eng.sem_inc(held, 1)

        JOBS = [[("A", 0), ("D", 0)], [("A", 1), ("D", 1)], [("A", 2)], [("A", 3), ("D", 2)], [("D", 3)],
                [("A", 4), ("D", 4)], [("A", 5)], []]

        def jobs_of(has_a, has_d):
            return [[j for j in slot if (has_a if j[0] == "A" else has_d)] for slot in JOBS]

        def c_par(k):
            return k % 2

        def run(eng, iteration):
            def one(it, static=None):
                k = it if static is None else static
                iteration(it, k, 0 <= k + 3 < NC, 0 <= k + 2 < NC, 0 <= k + 1 < NC, 0 <= k < NC, 0 <= k - 1 < NC)
            for it in range(-3, 1):
                one(it)
            loops = (NC - 4) // 2
            with eng.Fori(0, loops) as i:
                one(1 + 2 * i, 1)
                one(2 + 2 * i, 2)
            for it in range(1 + 2 * loops, NC + 1):
                one(it)

        block = ctx.enter_context(nc.Block())

        ONE = 1

        @block.sync
        def _(sp):
            sp.sem_inc(xn2_kept, ONE)
            for dst, src in [(ident[:], ident_c), (mask[:], head_mask_c), (inv_freq[:], inv_freq_c),
                             (pos_i[:], pos), (bk_col[:], bk), (ctxT, ctx_t.rearrange("(c p) m -> p c m", p=P)),
                             (wk_sb[:], wk.rearrange("(c p) e -> p c e", p=P)),
                             (wv_sb[:], wv.rearrange("(c p) e -> p c e", p=P)),
                             (wq_sb[:], wq.rearrange("(c p) e -> p c e", p=P)),
                             (wo_sb[:], wo.rearrange("(c p) e -> p c e", p=P)),
                             (gw_sb[:], gate_w.rearrange("(c p) e -> p c e", p=P)),
                             (bq_bc[:], bq.unsqueeze(0).to_broadcast([P, DM])),
                             (bv_bc[:], bv.unsqueeze(0).to_broadcast([P, DM])),
                             (bo_bc[:], bo.unsqueeze(0).to_broadcast([P, DM]))]:
                sp.dma_start(dst, src).then_inc(consts, 16)

            def load(c):
                sp.dma_start(xa[:, c, :, :], x1c[c]).then_inc(x_loaded, 16)

            def iteration(it, k, has_l, has_a, has_b, has_c, has_d):
                if has_l:
                    if k + 3 > 0:
                        sp.wait_ge(x_loaded, 16 * (it + 3))
                    load(it + 3)
                if has_d:
                    c = it - 1
                    sp.wait_ge(d_evac, DJ * c + 2)
                    sp.dma_start(x2c[c], xa[:, c, :, :]).then_inc(x2_stored, 16)
                    sp.wait_ge(xn2_ready, TI * c + TI)
                    sp.dma_start(xrow[:, bass.ds(c * TI, TI), 0:DM], xn2s[:]).then_inc(xn2_kept, 16)
            run(sp, iteration)
            sp.wait_ge(x2_stored, 16 * NC)
            sp.wait_ge(xn2_kept, ONE + 16 * NC)

        @block.gpsimd
        def _(pool):
            nc.gpsimd.memset(v_pad[:], 0.0).then_inc(v_zeroed, 1)

            def iteration(it, k, has_l, has_a, has_b, has_c, has_d):
                if has_c and k % CB == 0:
                    b = it // CB
                    pool.wait_ge(v_evac, 2 * NBR)
                    hold(pool, pv_done, NH * it)
                    nc.gpsimd.tensor_copy(v_cur[:], v_pad[:, b, :, :]).then_inc(v_copied, 1)

                def normalise(c, j):
                    hold(pool, rs_done, HT * c + j + 1)
                    v = probs[:, c_par(k + 1), j // 2, (j % 2) * HP * M:(j % 2 + 1) * HP * M] \
                        .rearrange("p (h m) -> p h m", m=M)
                    nc.gpsimd.tensor_tensor(v, v, rtotal[:, j % 4, :].unsqueeze(2).to_broadcast([P, HP, M]),
                                            ALU.mult).then_inc(norm_done, 1)

                def rope(c):
                    def half(t, n):
                        return t[:].rearrange("p i (h d) -> p i h d", d=HD)[:, :, :, n * HD // 2:(n + 1) * HD // 2]

                    def table(t):
                        return t[:, bass.ds(c * TI, TI), :].unsqueeze(2).to_broadcast([P, TI, NH, HD // 2])

                    n = 6 * c
                    pool.wait_ge(sin_done, 2)
                    hold(pool, a_evac, AJ * c + 4)
                    tt = nc.gpsimd.tensor_tensor
                    tt(rope_a[:], half(q, 0), table(cos_t), ALU.mult).then_inc(rope_step, 1)
                    hold(pool, rope_step, n + 1)
                    tt(rope_b[:], half(q, 1), table(sin_t), ALU.mult).then_inc(rope_step, 1)
                    hold(pool, rope_step, n + 2)
                    hold(pool, a_job, AJ * c)
                    tt(half(q_rot, 0), rope_a[:], rope_b[:], ALU.subtract).then_inc(rope_step, 1)
                    hold(pool, rope_step, n + 3)
                    tt(rope_a[:], half(q, 1), table(cos_t), ALU.mult).then_inc(rope_step, 1)
                    hold(pool, rope_step, n + 4)
                    tt(rope_b[:], half(q, 0), table(sin_t), ALU.mult).then_inc(rope_step, 1)
                    hold(pool, rope_step, n + 5)
                    tt(half(q_rot, 1), rope_a[:], rope_b[:], ALU.add).then_inc(rope_step, 1)

                if has_b:
                    for j in range(HT // 2):
                        normalise(it + 1, j)
                if has_a:
                    rope(it + 2)
                if has_b:
                    for j in range(HT // 2, HT):
                        normalise(it + 1, j)
                if has_c:
                    hold(pool, ln1, LN * it + LN)
                    hold(pool, xn_ready, TI * it + TI)
                    v = xa[:, it, :, :]
                    nc.gpsimd.tensor_tensor(v, v, bo_bc[:].unsqueeze(1).to_broadcast([P, TI, DM]),
                                            ALU.add).then_inc(bo_added, 1)
            run(pool, iteration)

        @block.scalar
        def _(act):
            act.wait_ge(consts, 16 * 14)
            for c in range(KD):
                act.wait_ge(k_done, c + 1)
                nc.scalar.activation(kT[:, c, :], ps[:, c, 0:NBR * M], ACT.Identity,
                                     bias=bk_col[:, c:c + 1]).then_inc(k_evac, 1)
            act.wait_ge(trig_step, 8)
            nc.scalar.activation(sin_t[:], ang[:], ACT.Sin).then_inc(sin_done, 1)
            act.wait_ge(trig_step, 10)
            nc.scalar.activation(cos_t[:], tmp_t[:], ACT.Sin).then_inc(sin_done, 1)

            def iteration(it, k, has_l, has_a, has_b, has_c, has_d):
                jobs = jobs_of(has_a, has_d)

                def exps(j):
                    c = it + 1
                    act.wait_ge(sub_done, HT * c + j + 1)
                    v = probs[:, c_par(k + 1), j // 2, (j % 2) * HP * M:(j % 2 + 1) * HP * M]
                    nc.scalar.activation(v, v, ACT.Exp, scale=SCALE).then_inc(exp_done, 1)

                def heads(h):
                    act.wait_ge(tr_done, NH * it + h + 1)
                    if not (k == 0 and h < 4):
                        act.wait_ge(pv_done, NH * it + h - 3)
                    nc.scalar.activation(pT[:, h % 4, :], ps[0:M, T_BANK + h % 2, :], ACT.Copy).then_inc(tr_evac, 1)

                for j in range(HT):
                    if has_b:
                        exps(j)
                    if has_c:
                        heads(2 * j)
                        if j == HT // 2:
                            act.wait_ge(pv_done, NH * it + HP)
                            nc.scalar.activation(oT[:, c_par(k), 0, :], ps[:, O_BANK, :], ACT.Copy).then_inc(o_evac, 1)
                        heads(2 * j + 1)
                    for kind, n in jobs[j]:
                        if kind == "A" and n in (0, 1, 4, 5):
                            act.wait_ge(a_job, AJ * (it + 2) + n + 1)
                            dst = xnT[:, n, :] if n < 2 else qT[:, c_par(k), n - 4, :]
                            nc.scalar.activation(dst, ps[:, JOB_BANK, :], ACT.Copy).then_inc(a_evac, 1)
                        elif kind == "D" and n in (2, 3):
                            act.wait_ge(d_job, DJ * (it - 1) + n + 1)
                            nc.scalar.activation(xn2T[:, n - 2, :], ps[:, JOB_BANK, :], ACT.Copy).then_inc(d_evac, 1)
                    if j == 1 and has_d:
                        act.wait_ge(ln2, LN * (it - 1) + LN)
                        nc.scalar.activation(rstd2[:], rstd2[:], ACT.Sqrt).then_inc(rstd2_ready, 1)
                    if j == HT - 2 and has_l:
                        act.wait_ge(ln1, LN * (it + 3) + LN)
                        nc.scalar.activation(rstd1[:], rstd1[:], ACT.Sqrt).then_inc(rstd1_ready, 1)
                if has_c:
                    act.wait_ge(pv_done, NH * it + NH)
                    nc.scalar.activation(oT[:, c_par(k), 1, :], ps[:, O_BANK, :], ACT.Copy).then_inc(o_evac, 1)
            run(act, iteration)

        @block.vector
        def _(dve):
            dve.wait_ge(consts, 16 * 14)
            def step(ins, n):
                ins.then_inc(trig_step, 1)
                dve.wait_ge(trig_step, n)

            v = nc.vector
            step(v.tensor_copy(pos_f[:], pos_i[:]), 1)
            step(v.tensor_tensor(ang[:], pos_f[:].unsqueeze(2).to_broadcast([P, NC * TI, HD // 2]),
                                 inv_freq[:].unsqueeze(1).to_broadcast([P, NC * TI, HD // 2]), ALU.mult), 2)
            step(v.tensor_scalar(turns[:], ang[:], 1 / TWO_PI, ROUND, ALU.mult, ALU.add), 3)
            step(v.tensor_scalar(turns[:], turns[:], ROUND, None, ALU.subtract), 4)
            for n, part in enumerate((C1, C2, C3)):
                step(v.scalar_tensor_tensor(out=ang[:], in0=turns[:], scalar=-part, in1=ang[:],
                                            op0=ALU.mult, op1=ALU.add), 5 + n)
            step(v.tensor_scalar(ang[:], ang[:], PI_IN, -PI_IN, ALU.min, ALU.max), 8)
            step(v.scalar_tensor_tensor(out=tmp_t[:], in0=ang[:], scalar=-1.0, in1=ang[:],
                                        op0=ALU.mult, op1=ALU.min), 9)
            step(v.tensor_scalar(tmp_t[:], tmp_t[:], np.pi / 2, None, ALU.add), 10)
            for c in range(KD):
                dve.wait_ge(k_evac, c + 1)
                for h in range(HP):
                    v.tensor_scalar(k_blk[:, c, :, h * M:(h + 1) * M], kT[:, c, :].rearrange("p (b m) -> p b m", m=M),
                                    mask[:, h:h + 1], None, ALU.mult).then_inc(k_blocks, 1)
            dve.wait_ge(k_blocks, KD * HP)
            dve.wait_ge(v_zeroed, 1)
            for b in range(NBR):
                dve.wait_ge(v_done, b + 1)
                for odd in range(2):
                    dst = v_pad[:, b, :, :].rearrange("m (g o) d -> m g o d", o=2)[:, :, odd, odd * HD:(odd + 1) * HD]
                    src = ps[0:M, 2 + b, 0:DM].rearrange("m (g o d) -> m g o d", o=2, d=HD)[:, :, odd, :]
                    bias = bv_bc[0:M, :].rearrange("m (g o d) -> m g o d", o=2, d=HD)[:, :, odd, :]
                    v.tensor_tensor(dst, src, bias, ALU.add).then_inc(v_evac, 1)

            def norm(c, xin, st, mv, rstd, chain, rstd_ready, out, ready):
                def first():
                    for i in range(TI):
                        v.bn_stats(st[:, i, :], xin(i)).then_inc(chain, 1)
                    for i in range(TI):
                        hold(dve, chain, LN * c + i + 1)
                        v.bn_aggr(mv[:, i, :], st[:, i, :]).then_inc(chain, 1)
                    dve.wait_ge(chain, LN * c + 2 * TI)
                    v.tensor_scalar(rstd[:], mv[:, :, 1], EPS, None, ALU.add).then_inc(chain, 1)
                    dve.wait_ge(chain, LN * c + 2 * TI + 1)
                    v.reciprocal(rstd[:], rstd[:]).then_inc(chain, 1)

                def second():
                    dve.wait_ge(chain, LN * c + 2 * TI)
                    dve.wait_ge(rstd_ready, c + 1)
                    for i in range(TI):
                        v.tensor_scalar(out(i), xin(i), mv[:, i, 0:1], rstd[:, i:i + 1],
                                        ALU.subtract, ALU.mult).then_inc(ready, 1)
                return first, second

            def iteration(it, k, has_l, has_a, has_b, has_c, has_d):
                jobs = jobs_of(has_a, has_d)
                if has_d:
                    d = it - 1
                    ln2_first, ln2_second = norm(d, lambda i: xa[:, d, i, :], stats2, mv2, rstd2, ln2, rstd2_ready,
                                                 lambda i: xn2s[:, i, :], xn2_ready)
                if has_l:
                    ln1_first, ln1_second = norm(it + 3, lambda i: xa[:, it + 3, i, :], stats, mv1, rstd1, ln1,
                                                 rstd1_ready, lambda i: xn[:, i, :], xn_ready)

                def scores(j):
                    c, par = it + 1, c_par(k + 1)
                    s = ps[:, S_BANK + 2 * (j % 2):S_BANK + 2 * (j % 2) + 2, 0:HM].rearrange("p a (h m) -> p a h m", m=M)
                    m2 = mx[:, j % 2, :].rearrange("p (a h) -> p a h", a=2)
                    out = probs[:, par, j // 2, (j % 2) * HP * M:(j % 2 + 1) * HP * M] \
                        .rearrange("p (a h m) -> p a h m", a=2, m=M)
                    dve.wait_ge(s_done, HT * c + j + 1)
                    v.reduce_max(m2, s, AXX).then_inc(mx_done, 1)
                    if k + 1 >= 2:
                        dve.wait_ge(tr_done, NH * (c - 1))
                    dve.wait_ge(mx_done, HT * c + j + 1)
                    v.tensor_tensor(out, s, m2.unsqueeze(3).to_broadcast([P, 2, HP // 2, M]),
                                    ALU.subtract).then_inc(sub_done, 1)

                def sums(j):
                    c, par = it + 1, c_par(k + 1)
                    src = probs[:, par, j // 2, (j % 2) * HP * M:(j % 2 + 1) * HP * M].rearrange("p (h m) -> p h m", m=M)
                    dve.wait_ge(exp_done, HT * c + j + 1)
                    v.reduce_sum(total[:, j % 2, :], src, AXX).then_inc(sum_done, 1)
                    if not (k + 1 == 0 and j < 4):
                        dve.wait_ge(norm_done, HT * c + j - 3)
                    dve.wait_ge(sum_done, HT * c + j + 1)
                    v.reciprocal(rtotal[:, j % 4, :], total[:, j % 2, :]).then_inc(rs_done, 1)

                for j in range(HT):
                    if has_b:
                        scores(j)
                        if j:
                            sums(j - 1)
                    for kind, n in jobs[j]:
                        if kind == "A" and n in (2, 3):
                            c = it + 2
                            dve.wait_ge(a_job, AJ * c + n + 1)
                            if k + 2 > 0:
                                dve.wait_ge(rope_step, 6 * c)
                            v.tensor_tensor(q[:, 2 * (n - 2):2 * (n - 2) + 2, :],
                                            ps[:, JOB_BANK, :].rearrange("p (i d) -> p i d", d=DM),
                                            bq_bc[:].unsqueeze(1).to_broadcast([P, 2, DM]),
                                            ALU.add).then_inc(a_evac, 1)
                        elif kind == "D" and n in (0, 1):
                            dve.wait_ge(d_job, DJ * d + n + 1)
                            dve.wait_ge(bo_added, d + 1)
                            xv = xa[:, d, 2 * n:2 * n + 2, :]
                            v.tensor_tensor(xv, ps[:, JOB_BANK, :].rearrange("p (i d) -> p i d", d=DM), xv,
                                            ALU.add).then_inc(d_evac, 1)
                        elif kind == "D" and n == 4:
                            dve.wait_ge(d_job, DJ * d + n + 1)
                            v.tensor_copy(logits[:, bass.ds(d * TI, TI), :],
                                          ps[:, JOB_BANK, 0:TI * E].rearrange("p (i e) -> p i e", e=E)).then_inc(d_evac, 1)
                    if j == 1 and has_d:
                        hold(dve, d_evac, DJ * d + 2)
                        ln2_first()
                    if j == 2 and has_d:
                        dve.wait_ge(xn2_kept, ONE + 16 * d)
                        ln2_second()
                    if j == HT - 2 and has_l:
                        hold(dve, x_loaded, 16 * (it + 4))
                        ln1_first()
                if has_b:
                    sums(HT - 1)
                if has_l:
                    dve.wait_ge(a_job, AJ * (it + 3) - 4 if has_a else 0)
                    ln1_second()
            run(dve, iteration)

        @block.tensor
        def _(pe):
            pe.wait_ge(consts, 16 * 14)
            t = nc.tensor
            for c in range(KD):
                for n in range(KD):
                    last = t.matmul(ps[:, c, 0:NBR * M], wk_sb[:, n, c * P:(c + 1) * P], ctxT[:, n, :],
                                    start=(n == 0), stop=(n == KD - 1))
                last.then_inc(k_done, 1)
            for b in range(NBR):
                for n in range(KD):
                    last = t.matmul(ps[0:M, 2 + b, 0:DM], ctxT[:, n, b * M:(b + 1) * M], wv_sb[:, n, :],
                                    start=(n == 0), stop=(n == KD - 1))
                last.then_inc(v_done, 1)
            pe.wait_ge(v_evac, 2 * NBR)
            pe.wait_ge(k_blocks, KD * HP)

            def iteration(it, k, has_l, has_a, has_b, has_c, has_d):
                jobs = jobs_of(has_a, has_d)
                order = [j for slot in jobs for j in slot]

                def bank_emptied(kind, n):
                    at = order.index((kind, n))
                    if at:
                        before, m = order[at - 1]
                        shift = 0
                    else:
                        was = [j for slot in jobs_of(0 <= k + 1 < NC, 0 <= k - 2 < NC) for j in slot]
                        if not was:
                            return
                        (before, m), shift = was[-1], -1
                    if before == "A":
                        pe.wait_ge(a_evac, AJ * (it + shift + 2) + m + 1)
                    else:
                        pe.wait_ge(d_evac, DJ * (it + shift - 1) + m + 1)

                def job(kind, n):
                    bank_emptied(kind, n)
                    out = ps[:, JOB_BANK, :]
                    if kind == "A":
                        c = it + 2
                        if n in (0, 1):
                            pe.wait_ge(xn_ready, TI * c + TI)
                            if n == 0 and k + 2 > 0:
                                hold(pe, a_job, AJ * c)
                            for i in range(TI):
                                last = t.transpose(out[:, i * P:(i + 1) * P], xn[:, i, n * P:(n + 1) * P], ident[:])
                        elif n in (2, 3):
                            pe.wait_ge(a_evac, AJ * c + 2)
                            for i in range(2):
                                tile = 2 * (n - 2) + i
                                for m in range(KD):
                                    last = t.matmul(out[:, i * DM:(i + 1) * DM], xnT[:, m, tile * P:(tile + 1) * P],
                                                    wq_sb[:, m, :], start=(m == 0), stop=(m == KD - 1))
                        else:
                            pe.wait_ge(rope_step, 6 * c + 6)
                            for i in range(TI):
                                last = t.transpose(out[:, i * P:(i + 1) * P], q_rot[:, i, (n - 4) * P:(n - 3) * P],
                                                   ident[:])
                        last.then_inc(a_job, 1)
                    else:
                        c, par = it - 1, c_par(k - 1)
                        if n in (0, 1):
                            pe.wait_ge(o_evac, 2 * c + 2)
                            for i in range(2):
                                tile = 2 * n + i
                                for m in range(KD):
                                    last = t.matmul(out[:, i * DM:(i + 1) * DM], oT[:, par, m, tile * P:(tile + 1) * P],
                                                    wo_sb[:, m, :], start=(m == 0), stop=(m == KD - 1))
                        elif n in (2, 3):
                            pe.wait_ge(xn2_ready, TI * c + TI)
                            for i in range(TI):
                                last = t.transpose(out[:, i * P:(i + 1) * P],
                                                   xn2s[:, i, (n - 2) * P:(n - 1) * P], ident[:])
                        else:
                            pe.wait_ge(d_evac, DJ * c + 4)
                            for i in range(TI):
                                for m in range(KD):
                                    last = t.matmul(out[:, i * E:(i + 1) * E], xn2T[:, m, i * P:(i + 1) * P],
                                                    gw_sb[:, m, :], start=(m == 0), stop=(m == KD - 1))
                        last.then_inc(d_job, 1)

                def scores(j):
                    c, par = it + 1, c_par(k + 1)
                    b = c // CB
                    if j == 0:
                        pe.wait_ge(a_evac, AJ * c + AJ)
                    if not (k + 1 == 0 and j < 2):
                        pe.wait_ge(sub_done, HT * c + j - 1)
                    i, hf = j // 2, j % 2
                    for a in range(2):
                        last = t.matmul(ps[:, S_BANK + 2 * (j % 2) + a, 0:HM], qT[:, par, hf, i * P:(i + 1) * P],
                                        k_blk[:, hf, b, a * HM:(a + 1) * HM], start=True, stop=True)
                    last.then_inc(s_done, 1)

                def turn(h):
                    pe.wait_ge(norm_done, HT * it + HT - 1 + h // HP)
                    if not (k == 0 and h < 2):
                        pe.wait_ge(tr_evac, NH * it + h - 1)
                    for i in range(TI):
                        last = t.transpose(ps[0:M, T_BANK + h % 2, i * P:(i + 1) * P],
                                           probs[:, c_par(k), i, h * M:(h + 1) * M], ident[:])
                    last.then_inc(tr_done, 1)

                def times_v(h):
                    pe.wait_ge(tr_evac, NH * it + h + 1)
                    if h == 0:
                        pe.wait_ge(v_copied, it // CB + 1)
                    if h % HP == 0 and not (k == 0 and h == 0):
                        pe.wait_ge(o_evac, 2 * it + h // HP)
                    g = h % HP // 2
                    t.matmul(ps[32 * g:32 * g + 32, O_BANK, :], v_cur[:, h, :], pT[:, h % 4, :],
                             start=(h % 2 == 0), stop=(h % 2 == 1)).then_inc(pv_done, 1)

                for j in range(HT):
                    if has_b:
                        scores(j)
                    if has_c:
                        turn(2 * j)
                        if j:
                            times_v(2 * j - 1)
                        turn(2 * j + 1)
                        times_v(2 * j)
                    for kind, n in jobs[j]:
                        job(kind, n)
                if has_c:
                    times_v(NH - 1)
            run(pe, iteration)


def dispatch_phase(nc, xrow, logits, lower_c, token_c, expert_c, tile_c, xs, tables, out):
    NT = xrow.shape[1]
    W = xrow.shape[2]
    E = logits.shape[2]
    D = W - E - PAD
    TILES = tables.shape[2]
    STRIDE = (xs.shape[0] - E * P) // E
    NTOK = NT * P

    with ExitStack() as ctx:
        def sb(name, shape, dt=F32):
            return ctx.enter_context(nc.sbuf_tensor(name, shape, dt))

        def sem(name):
            return ctx.enter_context(nc.semaphore(name))

        lower = sb("d_lower", [P, 2, P])
        token = sb("d_token", [P, NT + 1], I32)
        expert = sb("d_expert", [P, 3, E])
        tile_i = sb("d_tile", [1, TILES])
        p = sb("d_p", [P, NT, E])
        p2 = sb("d_p2", [P, NT, E])
        one1, one2 = sb("d_one1", [P, NT, E]), sb("d_one2", [P, NT, E])
        both = sb("d_both", [P, NT, E])
        cand = sb("d_cand", [P, NT, E])
        where = sb("d_where", [P, NT, E])
        upto = sb("d_upto", [P, NT, E])
        ones = sb("d_ones", [P, NT])
        row = {n: sb(f"d_{n}", [P, NT]) for n in ("m", "s", "r", "m1", "i1", "m2", "i2", "den", "w1", "w2", "pos1", "pos2")}
        pos_u = sb("d_pos_u", [P, 2, NT], U32)
        pad_f = sb("d_pad_f", [P, E])
        pad_p = sb("d_pad_p", [P, 1])
        pad_u = sb("d_pad_u", [P, E], U32)
        pad_row = sb("d_pad_row", [P, W])
        nt_f, nt_i = sb("d_nt_f", [P, E]), sb("d_nt_i", [P, E], I32)
        tend = sb("d_tend", [P, E])
        passed = sb("d_passed", [1, TILES, E])
        passed_n = sb("d_passed_n", [1, TILES, E])
        eid, first, eid7 = sb("d_eid", [1, TILES]), sb("d_first", [1, TILES]), sb("d_eid7", [1, TILES])
        ps = ctx.enter_context(nc.psum_tensor("d_ps", [P, 2, BANK], F32))

        consts, step, shifted, counted = sem("d_consts"), sem("d_step"), sem("d_shifted"), sem("d_counted")
        exp_done, padded, sent = sem("d_exp_done"), sem("d_padded"), sem("d_sent")
        placed, pads_placed, blank = sem("d_placed"), sem("d_pads_placed"), sem("d_blank")
        block = ctx.enter_context(nc.Block())

        def over_e(t):
            return t[:].unsqueeze(2).to_broadcast([P, NT, E])

        def over_t(t):
            return t.unsqueeze(1).to_broadcast([P, NT, E])

        @block.sync
        def _(sp):
            for dst, src in [(lower[:], lower_c), (token[:], token_c), (expert[:], expert_c), (tile_i[:], tile_c)]:
                sp.dma_start(dst, src).then_inc(consts, 16)
            sp.wait_ge(padded, 4)
            sp.dma_start(xs[E * STRIDE:E * STRIDE + E * P, :].rearrange("(k p) w -> p k w", p=P),
                         pad_row[:].unsqueeze(1).to_broadcast([P, E, W])).then_inc(blank, 16)
            sp.dma_start(out[NTOK:NTOK + P, :], pad_row[:, 0:D]).then_inc(blank, 16)
            sp.wait_ge(blank, 32)

        @block.gpsimd
        def _(pool):
            nc.gpsimd.memset(pad_row[:], 0.0).then_inc(padded, 1)
            nc.gpsimd.memset(ones[:], 1.0).then_inc(padded, 1)
            pool.wait_ge(consts, 64)
            pool.wait_ge(padded, 2)
            nc.gpsimd.tensor_copy(pad_row[:, D + E:D + E + 1].bitcast(I32), token[:, NT:NT + 1]).then_inc(padded, 1)
            nc.gpsimd.tensor_scalar(pad_p[:], token[:, NT:NT + 1], float(NTOK), None, ALU.subtract).then_inc(padded, 1)
            pool.wait_ge(placed, 1)
            pool.wait_ge(padded, 4)
            for i in range(NT):
                for k in range(2):
                    nc.gpsimd.indirect_dma_start(
                        out=xs, out_offset=bass.IndirectOffsetOnAxis(ap=pos_u[:, k, i:i + 1], axis=0),
                        in_=xrow[:, i, :], in_offset=None).then_inc(sent, 16)
            pool.wait_ge(pads_placed, 1)
            for e in range(E):
                nc.gpsimd.indirect_dma_start(
                    out=xs, out_offset=bass.IndirectOffsetOnAxis(ap=pad_u[:, e:e + 1], axis=0),
                    in_=pad_row[:], in_offset=None).then_inc(sent, 16)
            pool.wait_ge(sent, 16 * (2 * NT + E))

        @block.scalar
        def _(act):
            act.wait_ge(shifted, 1)
            nc.scalar.activation(p[:], p[:], ACT.Exp).then_inc(exp_done, 1)

        @block.tensor
        def _(pe):
            pe.wait_ge(consts, 64)
            pe.wait_ge(counted, 1)
            for k in range(2):
                last = nc.tensor.matmul(ps[:, k, 0:NT * E], lower[:, k, :], both[:].rearrange("p t e -> p (t e)"),
                                        start=True, stop=True)
            last.then_inc(counted, 1)

        @block.vector
        def _(dve):
            v = nc.vector
            n = [0]

            def then(ins):
                n[0] += 1
                ins.then_inc(step, 1)
                dve.wait_ge(step, n[0])

            dve.wait_ge(consts, 64)
            dve.wait_ge(padded, 4)
            then(v.reduce_max(row["m"][:], logits[:], AXX))
            v.tensor_tensor(p[:], logits[:], over_e(row["m"]), ALU.subtract).then_inc(shifted, 1)
            dve.wait_ge(exp_done, 1)
            then(v.reduce_sum(row["s"][:], p[:], AXX))
            then(v.reciprocal(row["r"][:], row["s"][:]))
            then(v.tensor_tensor(p[:], p[:], over_e(row["r"]), ALU.mult))

            def choose(src, m, i, one):
                then(v.reduce_max(row[m][:], src[:], AXX))
                then(v.tensor_tensor(cand[:], src[:], over_e(row[m]), ALU.is_equal))
                then(v.scalar_tensor_tensor(out=cand[:], in0=cand[:], scalar=-float(E), in1=over_t(expert[:, 1, :]),
                                            op0=ALU.mult, op1=ALU.add))
                then(v.tensor_reduce(row[i][:], cand[:], AXX, ALU.min))
                then(v.tensor_tensor(one[:], over_t(expert[:, 0, :]), over_e(row[i]), ALU.is_equal))

            choose(p, "m1", "i1", one1)
            then(v.scalar_tensor_tensor(out=p2[:], in0=one1[:], scalar=-2.0, in1=p[:], op0=ALU.mult, op1=ALU.add))
            choose(p2, "m2", "i2", one2)
            v.tensor_tensor(both[:], one1[:], one2[:], ALU.add).then_inc(counted, 1)
            then(v.tensor_tensor(row["den"][:], row["m1"][:], row["m2"][:], ALU.add))
            then(v.reciprocal(row["den"][:], row["den"][:]))
            then(v.tensor_tensor(row["w1"][:], row["m1"][:], row["den"][:], ALU.mult))
            then(v.tensor_tensor(row["w2"][:], row["m2"][:], row["den"][:], ALU.mult))
            then(v.tensor_tensor(cand[:], one1[:], over_e(row["w1"]), ALU.mult))
            then(v.tensor_tensor(p2[:], one2[:], over_e(row["w2"]), ALU.mult))
            then(v.tensor_tensor(xrow[:, :, D:D + E], cand[:], p2[:], ALU.add))
            then(v.tensor_copy(xrow[:, :, D + E:D + E + 1].bitcast(I32), token[:, 0:NT].unsqueeze(2)))
            then(v.memset(xrow[:, :, D + E + 1:W], 0.0))
            dve.wait_ge(counted, 2)
            tot = ps[:, 1, 0:NT * E].rearrange("p (t e) -> p t e", e=E)
            for e in range(E):
                then(v.tensor_tensor_scan(upto[:, :, e], ones[:], tot[:, :, e], 0.0, ALU.mult, ALU.add))
            then(v.tensor_tensor(where[:], upto[:], tot, ALU.subtract))
            then(v.tensor_tensor(where[:], ps[:, 0, 0:NT * E].rearrange("p (t e) -> p t e", e=E), where[:], ALU.add))
            then(v.tensor_tensor(where[:], where[:], over_t(expert[:, 2, :]), ALU.add))
            for k, (one, pos) in enumerate(((one1, "pos1"), (one2, "pos2"))):
                then(v.tensor_tensor(cand[:], one[:], where[:], ALU.mult))
                then(v.reduce_sum(row[pos][:], cand[:], AXX))
                if k == 0:
                    then(v.tensor_copy(pos_u[:, k, :], row[pos][:]))
                else:
                    v.tensor_copy(pos_u[:, k, :], row[pos][:]).then_inc(placed, 1)
            count = upto[:, NT - 1, :]
            then(v.scalar_tensor_tensor(out=pad_f[:], in0=count, scalar=pad_p[:, 0:1], in1=expert[:, 2, :],
                                        op0=ALU.add, op1=ALU.add))
            v.tensor_copy(pad_u[:], pad_f[:]).then_inc(pads_placed, 1)
            then(v.tensor_scalar(nt_f[:], count, float(P - 1), None, ALU.add))
            then(v.tensor_copy(nt_i[:], nt_f[:]))
            then(v.tensor_scalar(nt_i[:], nt_i[:], 7, None, ALU.arith_shift_right))
            then(v.tensor_copy(nt_f[:], nt_i[:]))
            then(v.tensor_tensor_scan(tend[:], ones[:, 0:E], nt_f[:], 0.0, ALU.mult, ALU.add))
            tiles3 = [1, TILES, E]
            then(v.tensor_tensor(passed[:], tile_i[:].unsqueeze(2).to_broadcast(tiles3),
                                 tend[0:1, :].unsqueeze(1).to_broadcast(tiles3), ALU.is_ge))
            then(v.reduce_sum(eid[:], passed[:], AXX))
            then(v.tensor_tensor(passed_n[:], passed[:], nt_f[0:1, :].unsqueeze(1).to_broadcast(tiles3), ALU.mult))
            then(v.reduce_sum(first[:], passed_n[:], AXX))
            then(v.tensor_tensor(first[:], tile_i[:], first[:], ALU.subtract))
            then(v.tensor_scalar(first[:], first[:], float(P), None, ALU.mult))
            then(v.scalar_tensor_tensor(out=first[:], in0=eid[:], scalar=float(STRIDE), in1=first[:],
                                        op0=ALU.mult, op1=ALU.add))
            then(v.tensor_copy(tables[:, 0, :], first[:]))
            then(v.tensor_scalar(eid7[:], eid[:], float(E - 1), None, ALU.min))
            then(v.tensor_copy(tables[:, 1, :], eid7[:]))
            then(v.tensor_scalar(tables[:, 2, :], tables[:, 1, :], SLOTS - 1, None, ALU.bitwise_and))
            then(v.tensor_scalar(eid7[:], eid7[:], float(LOADS), float(LOADS), ALU.mult, ALU.add))
            then(v.tensor_copy(tables[:, 4, :], eid7[:]))
            then(v.tensor_scalar(eid[:, 0:E], tend[0:1, :], 1.0, None, ALU.add))
            then(v.tensor_copy(tables[:, 3, 0:E], eid[:, 0:E]))


def experts_phase(nc, xs, tables, gate_up_w, down_w, ident_c, out):
    W = xs.shape[1]
    E, D, F2 = gate_up_w.shape
    F = F2 // 2
    TILES = tables.shape[2]
    KD, KF = D // P, F // P
    NROWS = out.shape[0]
    U = 4

    with ExitStack() as ctx:
        def sb(name, shape, dt=F32):
            return ctx.enter_context(nc.sbuf_tensor(name, shape, dt))

        def sem(name):
            return ctx.enter_context(nc.semaphore(name))

        ident = sb("e_ident", [P, P])
        w1 = sb("e_w1", [P, SLOTS, KD, F2])
        w2 = sb("e_w2", [P, SLOTS, KF, D])
        xg = sb("e_xg", [P, U, W])
        xT = sb("e_xT", [P, 2, KD, P])
        gact = sb("e_gact", [P, 2, BANK])
        hact = sb("e_hact", [P, 2, F])
        hT = sb("e_hT", [P, 2, KF, P])
        y = sb("e_y", [P, 2, D])
        ps = ctx.enter_context(nc.psum_tensor("e_ps", [P, 8, BANK], F32))
        T_BANK, Y_BANK, X_BANK = 4, 6, 7

        consts = sem("e_consts")
        w_loaded = sem("e_w_loaded")
        x_loaded = [sem(f"e_x_loaded{i}") for i in range(U)]
        x_turned, xT_ready = sem("e_x_turned"), sem("e_xT_ready")
        gu_done, g_ready, h_ready = sem("e_gu_done"), sem("e_g_ready"), sem("e_h_ready")
        h_turned, hT_ready = sem("e_h_turned"), sem("e_hT_ready")
        y_done, y_ready, added = sem("e_y_done"), sem("e_y_ready"), sem("e_added")
        held = sem("e_held")

        def hold(eng, of, value):
            eng.wait_ge(of, value)
            eng.sem_inc(held, 1)

        def groups(eng, body):
            n = TILES // U
            for j in range(U):
                body(j, 0, j, j == 0, False)
            with eng.Fori(1, n - 1) as g:
                for j in range(U):
                    body(U * g + j, g, j, False, False)
            for j in range(U):
                i = TILES - U + j
                body(i, n - 1, j, False, i + 1 == TILES)

        block = ctx.enter_context(nc.Block())

        ONE = 1

        @block.sync
        def _(sp):
            sp.sem_inc(y_done, ONE)
            for e in range(E):
                s = e % SLOTS
                if e >= SLOTS:
                    end = sp.value_load(tables[0:1, 3, e - SLOTS:e - SLOTS + 1], min_val=1, max_val=TILES + 1)
                    sp.wait_ge(y_done, end)
                if e:
                    sp.wait_ge(w_loaded, LOADS * e)
                for c in range(KD):
                    sp.dma_start(w1[:, s, c, :], gate_up_w[e, c * P:(c + 1) * P, :]).then_inc(w_loaded, 16)
                sp.dma_start(w2[:, s, :, :], down_w[e].rearrange("(c p) d -> p c d", p=P)).then_inc(w_loaded, 16)
            sp.wait_ge(added, 16 * TILES)

        @block.gpsimd
        def _(pool):
            nc.gpsimd.dma_start(ident[:], ident_c).then_inc(consts, 16)

            def load(i, j):
                row = pool.value_load(tables[0:1, 0, bass.ds(i, 1)], min_val=0, max_val=xs.shape[0] - P)
                nc.gpsimd.dma_start(xg[:, j % U, :], xs[bass.ds(row, P), :]).then_inc(x_loaded[j % U], 16)

            for j in range(U - 1):
                load(j, j)

            def tile(i, g, j, first, last):
                hold(pool, y_ready, i + 1)
                if not first:
                    hold(pool, added, 16 * i)
                nc.gpsimd.indirect_dma_start(
                    out=out, out_offset=bass.IndirectOffsetOnAxis(ap=xg[:, j, D + E:D + E + 1].bitcast(U32), axis=0),
                    in_=y[:, j % 2, :], in_offset=None, compute_op=ALU.add).then_inc(added, 16)
                if not isinstance(i, int) or i + U - 1 < TILES:
                    load(i + U - 1, j + U - 1)
            groups(pool, tile)

        @block.scalar
        def _(act):
            def turn_x(i, j):
                act.wait_ge(x_turned, i + 1)
                nc.scalar.activation(xT[:, j % 2, :, :].rearrange("p c t -> p (c t)"), ps[:, X_BANK, 0:D],
                                     ACT.Copy).then_inc(xT_ready, 1)

            def gelu(i, h):
                act.wait_ge(gu_done, 2 * i + h + 1)
                nc.scalar.activation(gact[:, h, :], ps[:, 2 * h, :], ACT.Gelu).then_inc(g_ready, 1)

            def turn_h(i, j, h):
                act.wait_ge(h_turned, 2 * i + h + 1)
                nc.scalar.activation(hT[:, j % 2, h * KF // 2:(h + 1) * KF // 2, :].rearrange("p c t -> p (c t)"),
                                     ps[:, T_BANK + h, :], ACT.Copy).then_inc(hT_ready, 1)

            turn_x(0, 0)

            def tile(i, g, j, first, last):
                if not first:
                    act.wait_ge(h_ready, 2 * i)
                gelu(i, 0)
                if not first:
                    turn_h(i - 1, j - 1, 1)
                gelu(i, 1)
                if not (isinstance(i, int) and i < 2):
                    act.wait_ge(y_done, ONE + i - 1)
                turn_h(i, j, 0)
                if not last:
                    turn_x(i + 1, j + 1)
            groups(act, tile)
            turn_h(TILES - 1, U - 1, 1)

        @block.vector
        def _(dve):
            def weigh(i, j, e):
                dve.wait_ge(y_done, ONE + i + 1)
                if not (isinstance(i, int) and i < 2):
                    dve.wait_ge(added, 16 * (i - 1))
                nc.vector.tensor_scalar(y[:, j % 2, :], ps[:, Y_BANK, 0:D], xg[:, j % U, bass.ds(D + e, 1)], None,
                                        ALU.mult).then_inc(y_ready, 1)

            def tile(i, g, j, first, last):
                for h in range(2):
                    dve.wait_ge(g_ready, 2 * i + h + 1)
                    if not (isinstance(i, int) and i < 2):
                        dve.wait_ge(h_turned, 2 * (i - 1))
                    nc.vector.tensor_tensor(hact[:, j % 2, h * BANK:(h + 1) * BANK], gact[:, h, :],
                                            ps[:, 2 * h + 1, :], ALU.mult).then_inc(h_ready, 1)
                if not first:
                    weigh(i - 1, j - 1, expert(i - 1))

            def expert(i):
                return dve.value_load(tables[0:1, 1, bass.ds(i, 1)], min_val=0, max_val=E - 1)
            groups(dve, tile)
            weigh(TILES - 1, U - 1, expert(TILES - 1))

        @block.tensor
        def _(pe):
            t = nc.tensor
            pe.wait_ge(consts, 16)

            def turn_x(i, j, g):
                pe.wait_ge(x_loaded[j % U], 16 * g + 16)
                if not (isinstance(i, int) and i == 0):
                    pe.wait_ge(xT_ready, i)
                for c in range(KD):
                    last = t.transpose(ps[:, X_BANK, c * P:(c + 1) * P], xg[:, j % U, c * P:(c + 1) * P], ident[:])
                last.then_inc(x_turned, 1)

            def gate_up(i, j, h, slot):
                if not (isinstance(i, int) and i == 0):
                    pe.wait_ge(h_ready, 2 * i + h - 1)
                for which in range(2):
                    lo = which * F + h * BANK
                    for c in range(KD):
                        last = t.matmul(ps[:, 2 * h + which, :], xT[:, j % 2, c, :],
                                        w1[:, bass.ds(slot, 1), c, lo:lo + BANK].rearrange("p a n -> p (a n)"),
                                        start=(c == 0), stop=(c == KD - 1))
                last.then_inc(gu_done, 1)

            def turn_h(i, j, h):
                pe.wait_ge(h_ready, 2 * i + h + 1)
                if not (isinstance(i, int) and i == 0):
                    pe.wait_ge(hT_ready, 2 * i + h - 1)
                for c in range(KF // 2):
                    lo = h * BANK + c * P
                    last = t.transpose(ps[:, T_BANK + h, c * P:(c + 1) * P], hact[:, j % 2, lo:lo + P], ident[:])
                last.then_inc(h_turned, 1)

            def down(i, j, slot):
                pe.wait_ge(hT_ready, 2 * i + 2)
                if not (isinstance(i, int) and i == 0):
                    pe.wait_ge(y_ready, i)
                for c in range(KF):
                    last = t.matmul(ps[:, Y_BANK, 0:D], hT[:, j % 2, c, :],
                                    w2[:, bass.ds(slot, 1), c, :].rearrange("p a n -> p (a n)"),
                                    start=(c == 0), stop=(c == KF - 1))
                last.then_inc(y_done, 1)

            def entry(k, i, most):
                return pe.value_load(tables[0:1, k, bass.ds(i, 1)], min_val=0, max_val=most)

            turn_x(0, 0, 0)

            def tile(i, g, j, first, last):
                slot = entry(2, i, SLOTS - 1)
                pe.wait_ge(w_loaded, pe.value_load(tables[0:1, 4, bass.ds(i, 1)], min_val=LOADS, max_val=LOADS * E))
                pe.wait_ge(xT_ready, i + 1)
                gate_up(i, j, 0, slot)
                if not first:
                    turn_h(i - 1, j - 1, 1)
                gate_up(i, j, 1, slot)
                if not first:
                    down(i - 1, j - 1, entry(2, i - 1, SLOTS - 1))
                turn_h(i, j, 0)
                if not last:
                    turn_x(i + 1, j + 1, g + (j + 1) // U)
            groups(pe, tile)
            turn_h(TILES - 1, U - 1, 1)
            down(TILES - 1, U - 1, entry(2, TILES - 1, SLOTS - 1))


def decoder_layer(nc, a, out):
    NB, T, DM = a["x"].shape
    N = a["a_log"].shape[1]
    NTOK = NB * T
    E, F2 = a["gate_up_w"].shape[0], a["gate_up_w"].shape[2]
    TILES = a["tile_c"].shape[1]
    NT = NTOK // P
    W = DM + E + PAD
    c_rows = nc.dram_tensor("c_rows", (NB, N, T), F32).ap()
    x1 = nc.dram_tensor("x1", (NB, T, DM), F32).ap()
    xs = nc.dram_tensor("routed_rows", (E * list_stride(NTOK) + E * P, W), F32).ap()
    x2 = out[0:NTOK, :].rearrange("(b t) d -> b t d", b=NB)
    mamba_phase(nc, a["x"], a["in_w"], a["conv_w"], a["xproj_w"], a["dtproj_w"], a["dtproj_b"], a["a_log"],
                a["d_vec"], a["out_w"], a["ident"], a["sel"], c_rows, x1)
    with nc.sbuf_tensor("tables", [1, 5, TILES], I32) as tables:
        with nc.sbuf_tensor("xrow", [P, NT, W], F32) as xrow, nc.sbuf_tensor("logits", [P, NT, E], F32) as logits:
            attention_phase(nc, x1, a["ctx_t"], a["pos"], a["wq"], a["wk"], a["wv"], a["wo"], a["bq"], a["bk"],
                            a["bv"], a["bo"], a["ident"], a["head_mask"], a["inv_freq"], a["gate_w"],
                            x2, xrow, logits)
            dispatch_phase(nc, xrow, logits, a["lower"], a["token"], a["expert"], a["tile_c"], xs, tables, out)
        experts_phase(nc, xs, tables, a["gate_up_w"], a["down_w"], a["ident"], out)


def list_stride(tokens):
    return tokens + P


def kernel(**inputs):
    import concourse.bacc as bacc
    from concourse.bass_utils import run_bass_kernel_spmd

    i = {k: np.asarray(v) for k, v in inputs.items()}
    B, T, D = i["x"].shape
    ED, _, KC = i["L0_attn_conv_w"].shape
    N = i["L0_attn_A_log"].shape[1]
    E = i["L0_ffn_gate_w"].shape[0]
    HD = 16
    NTOK = B * T
    NT = NTOK // P
    TILES = 2 * NT + E
    f32 = np.float32
    sel = np.zeros((96, N, P), f32)
    for n in range(N):
        sel[n::32, n] = 1
    sel[16:32] = sel[48:64] = sel[80:96] = 0
    inv_freq = (f32(1) / f32(10000) ** (np.arange(0, HD, 2, dtype=f32) / f32(HD))).astype(f32)
    e = np.arange(E)
    arrays = dict(
        x=i["x"], in_w=i["L0_attn_in_proj_w"].T, conv_w=i["L0_attn_conv_w"][:, 0, :], xproj_w=i["L0_attn_x_proj_w"].T,
        dtproj_w=i["L0_attn_dt_proj_w"].T, dtproj_b=i["L0_attn_dt_proj_b"].reshape(ED // P, P).T,
        a_log=i["L0_attn_A_log"], d_vec=i["L0_attn_D"].reshape(ED // P, P).T, out_w=i["L0_attn_out_proj_w"].T,
        ident=np.eye(P, dtype=f32), sel=sel.reshape(96, N * P),
        ctx_t=i["ctx_1024"].reshape(-1, D).T, pos=i["itok_BxS_1_4095"].reshape(NT, P).T,
        wq=i["L0_xattn_Wq"].T, wk=i["L0_xattn_Wk"].T, wv=i["L0_xattn_Wv"].T, wo=i["L0_xattn_Wo"].T,
        bq=i["L0_xattn_bq"], bk=i["L0_xattn_bk"].reshape(D // P, P).T, bv=i["L0_xattn_bv"], bo=i["L0_xattn_bo"],
        head_mask=(np.arange(P)[:, None] // HD == np.arange(P // HD)).astype(f32),
        inv_freq=np.tile(inv_freq, (P, 1)), gate_w=i["L0_ffn_gate_w"].T,
        lower=np.stack([np.triu(np.ones((P, P), f32), 1), np.ones((P, P), f32)], 1),
        token=(np.arange(NT + 1) * P + np.arange(P)[:, None]).astype(np.int32),
        expert=np.tile(np.stack([e, e + E, e * list_stride(NTOK)]).astype(f32), (P, 1, 1)),
        tile_c=np.arange(TILES, dtype=f32)[None],
        gate_up_w=i["L0_ffn_gate_up_w"].transpose(0, 2, 1), down_w=i["L0_ffn_down_w"].transpose(0, 2, 1),
    )
    arrays = {k: np.ascontiguousarray(v) for k, v in arrays.items()}
    nc = bacc.Bacc("TRN2", target_bir_lowering=False, num_devices=1)
    aps = {k: nc.dram_tensor(f"in_{k}", v.shape, mybir.dt.from_np(v.dtype), kind="ExternalInput").ap()
           for k, v in arrays.items()}
    out = nc.dram_tensor("out_0", (NTOK + P, D), F32, kind="ExternalOutput").ap()
    decoder_layer(nc, aps, out)
    r = run_bass_kernel_spmd(nc, [{f"in_{k}": v for k, v in arrays.items()}], core_ids=[0])
    return r.results[0]["out_0"][0:NTOK].reshape(B, T, D)
```

```python
import numpy as np
import concourse.bass as bass
from concourse import mybir
from contextlib import ExitStack

F32, BF16, I32, U32 = mybir.dt.float32, mybir.dt.bfloat16, mybir.dt.int32, mybir.dt.uint32
ACT = mybir.ActivationFunctionType
ALU = mybir.AluOpType
AXX = mybir.AxisListType.X
P = 128
BANK = 512
EPS = 1e-5
EXP_LN = "natural_log_exp_and_others"

SLOTS = 4
LOADS = 48

def mamba_phase(nc, x, in_w, conv_w, xproj_w, dtproj_w, dtproj_b, a_log, d_vec, out_w, ident_c, sel_c, c_rows_dram, x1):
    NB, T, DM = x.shape
    ED, KC = conv_w.shape
    N = a_log.shape[1]
    R = dtproj_w.shape[0]
    KD = DM // P
    KE = ED // P
    NT = T // P
    H = T // BANK
    LAG = 4
    HC_AT = KE * T + 16

    with ExitStack() as ctx:
        def sb(name, shape, dt=F32):
            return ctx.enter_context(nc.sbuf_tensor(name, shape, dt))

        def sem(name):
            return ctx.enter_context(nc.semaphore(name))

        ident = sb("m_ident", [P, P])
        w_in = sb("m_w_in", [P, KD, 2 * ED])
        w_x = sb("m_w_x", [P, KE, 3 * N + N + R])
        w_dt = sb("m_w_dt", [P, ED])
        w_out = sb("m_w_out", [P, KE, DM])
        wconv = sb("m_wconv", [P, KE, KC])
        b_dt = sb("m_b_dt", [P, KE])
        negA = sb("m_negA", [P, KE, N])
        dvec = sb("m_dvec", [P, KE])
        sel = sb("m_sel", [3 * N, N, P], BF16)
        xn = sb("m_xn", [P, NT, DM])
        x_res = sb("m_x_res", [P, NT, DM])
        stats = sb("m_stats", [P, NT, 6])
        mv = sb("m_mv", [P, NT, 2])
        rstd = sb("m_rstd", [P, NT])
        silu_z = sb("m_silu_z", [P, KE, T])
        xc = sb("m_xc", [P, KE, T])
        delta = sb("m_delta", [P, KE, T])
        u = sb("m_u", [P, KE, T])
        c_bc = sb("m_c_bc", [P, N, T])
        b_split = sb("m_b_split", [3 * N, T], BF16)
        AH, HC = 2, 4
        region = sb("m_region", [P, HC_AT + HC * T])
        a_ring = [region[:, i * T:(i + 1) * T] for i in range(AH)]
        h_ring = [region[:, (AH + i) * T:(AH + i + 1) * T] for i in range(AH)]
        hc_ring = [region[:, HC_AT + i * T:HC_AT + (i + 1) * T] for i in range(HC)]
        XPW = T + KC - 1
        xp = region[:, 0:KE * XPW].rearrange("p (c t) -> p c t", c=KE)
        xnT = region[:, HC_AT:HC_AT + KD * T].rearrange("p (c t) -> p c t", c=KD)
        xd_rows = region[:, HC_AT:HC_AT + T]
        b_res = region[0:2 * N, HC_AT + T:HC_AT + 2 * T]
        C0, DT0 = 3 * N, 4 * N
        ps = ctx.enter_context(nc.psum_tensor("m_ps", [P, 8, BANK], F32))
        sel_stage = silu_z[0:3 * N, 0:2, :].rearrange("p a (n m) -> p (a n) m", m=P)

        def pair_of_banks(k):
            return ps[:, 2 * k:2 * k + 2, :].rearrange("p a t -> p (a t)")

        Y_PAIR = 3
        B_PAIR = [n % 3 for n in range(N - 1)] + [1]
        B_AGO = []
        for n in range(N):
            ago = 1
            while B_PAIR[(n - ago) % N] != B_PAIR[n]:
                ago += 1
            B_AGO.append(ago)
        AGO = max(B_AGO)

        w_in_loaded = sem("m_w_in_loaded")
        consts = sem("m_consts")
        pads = sem("m_pads")
        sel_ready = sem("m_sel_ready")
        negA_ready = sem("m_negA_ready")
        x_loaded = sem("m_x_loaded")
        res_loaded = sem("m_res_loaded")
        dve_ln = sem("m_dve_ln")
        log_ready, rstd_ready = sem("m_log_ready"), sem("m_rstd_ready")
        xn_ready = sem("m_xn_ready")
        proj_done = sem("m_proj_done")
        evac_done = sem("m_evac_done")
        conv_step = sem("m_conv_step")
        conv_done = sem("m_conv_done")
        silu_done = sem("m_silu_done")
        b_rounded = sem("m_b_rounded")
        b_sub = sem("m_b_sub")
        c_stored = sem("m_c_stored")
        cb_loaded = [sem(f"m_cb_loaded{g}") for g in range(4)]
        neg_abs = sem("m_neg_abs")
        exp1_done = sem("m_exp1_done")
        ln_done = sem("m_ln_done")
        delta_done = sem("m_delta_done")
        u_done = sem("m_u_done")
        bcast_done = sem("m_bcast_done")
        a_ready = sem("m_a_ready")
        bx_done = sem("m_bx_done")
        scan_done = sem("m_scan_done")
        hc_done = sem("m_hc_done")
        yacc_done = sem("m_yacc_done")
        y_read = sem("m_y_read")
        gated = sem("m_gated")
        out_done = sem("m_out_done")
        res_done = sem("m_res_done")
        x1_stored = sem("m_x1_stored")
        held = sem("m_held")

        def hold(eng, of, value):
            eng.wait_ge(of, value)
            eng.sem_inc(held, 1)

        G = 4
        OTHERS = 12
        J_IN, J_X = KD * H, KD * H + 2 * KE * H
        J_DT = J_X + H
        JOBS = J_DT + KE * H
        STEPS = KE * N
        LN_STEPS = 2 * NT + 1

        ONE = 1

        block = ctx.enter_context(nc.Block())

        @block.sync
        def _(sp):
            for s in (res_done, y_read, gated, x1_stored):
                sp.sem_inc(s, ONE)
            sp.dma_start(xn[:], x[0].rearrange("(i p) d -> p i d", p=P)).then_inc(x_loaded, 16)
            sp.dma_start(ident[:], ident_c).then_inc(w_in_loaded, 16)
            sp.dma_start(w_in[:], in_w.rearrange("(c p) e -> p c e", p=P)).then_inc(w_in_loaded, 16)
            xw = xproj_w.rearrange("(c p) f -> p c f", p=P)
            for dst, src in [(sel_stage, sel_c.rearrange("k (n m) -> k n m", m=P)),
                             (wconv[:], conv_w.rearrange("(c p) k -> p c k", p=P)),
                             (w_x[:, :, 0:N], xw[:, :, R:R + N]), (w_x[:, :, N:2 * N], xw[:, :, R:R + N]),
                             (w_x[:, :, 2 * N:3 * N], xw[:, :, R:R + N]),
                             (w_x[:, :, C0:C0 + N], xw[:, :, R + N:R + 2 * N]),
                             (w_x[:, :, DT0:DT0 + R], xw[:, :, 0:R]),
                             (w_dt[DT0:DT0 + R, :], dtproj_w), (b_dt[:], dtproj_b),
                             (negA[:], a_log.rearrange("(c p) n -> p c n", p=P)), (dvec[:], d_vec),
                             (w_out[:], out_w.rearrange("(c p) d -> p c d", p=P))]:
                sp.dma_start(dst, src).then_inc(consts, 16)

            def row(b, last):
                sp.wait_ge(x1_stored, ONE + 16 * b)
                sp.dma_start(x_res[:], x[b].rearrange("(i p) d -> p i d", p=P)).then_inc(res_loaded, 16)
                if not last:
                    sp.wait_ge(proj_done, JOBS * b + J_IN)
                    sp.dma_start(xn[:], x[b + 1].rearrange("(i p) d -> p i d", p=P)).then_inc(x_loaded, 16)
                sp.wait_ge(evac_done, JOBS * b + J_X + H)
                sp.dma_start(c_rows_dram[b], xd_rows[C0:C0 + N, :]).then_inc(c_stored, 16)
                sp.wait_ge(c_stored, 16 * b + 16)
                sp.wait_ge(hc_done, AH + STEPS * b)
                for g in range(G):
                    src = c_rows_dram[b, g * (N // G):(g + 1) * (N // G), :]
                    sp.dma_start(c_bc[:, g * (N // G):(g + 1) * (N // G), :],
                                 src.unsqueeze(0).to_broadcast([P, N // G, T])).then_inc(cb_loaded[g], 16)
                sp.wait_ge(res_done, ONE + NT * b + NT)
                sp.dma_start(x1[b].rearrange("(i p) d -> p i d", p=P), x_res[:]).then_inc(x1_stored, 16)

            with sp.Fori(0, NB - 1) as b:
                row(b, False)
            row(NB - 1, True)
            sp.wait_ge(x1_stored, ONE + 16 * NB)

        @block.gpsimd
        def _(pool):
            pool.wait_ge(consts, 16 * OTHERS)
            nc.gpsimd.tensor_copy(sel[:], sel_stage).then_inc(sel_ready, 1)
            nc.gpsimd.sem_inc(hc_done, AH)
            with pool.Fori(0, NB) as b:
                hold(pool, yacc_done, HC + STEPS * b)
                nc.gpsimd.memset(xp[:, :, 0:KC - 1], 0.0).then_inc(pads, 1)
                pool.wait_ge(b_rounded, 3 * b + 1)
                nc.gpsimd.tensor_tensor(b_res, xd_rows[0:2 * N, :], b_split[0:2 * N, :],
                                        ALU.subtract).then_inc(b_sub, 1)
                pool.wait_ge(b_sub, 2 * b + 1)
                pool.wait_ge(b_rounded, 3 * b + 2)
                nc.gpsimd.tensor_tensor(b_res[0:N, :], b_res[0:N, :], b_split[0:N, :],
                                        ALU.subtract).then_inc(b_sub, 1)
                hold(pool, b_rounded, 3 * b + 3)
                hold(pool, c_stored, 16 * b + 16)
                hold(pool, proj_done, JOBS * b + JOBS)
                with pool.Fori(0, KE) as e:
                    for n in range(N):
                        s = b * STEPS + e * N + n
                        if n % (N // G) == 0:
                            pool.wait_ge(cb_loaded[n // (N // G)], 16 * b + 16)
                        pool.wait_ge(scan_done, AGO + 1 + s)
                        pool.wait_ge(yacc_done, 1 + s)
                        nc.gpsimd.tensor_tensor(hc_ring[n % HC], h_ring[n % AH], c_bc[:, n, :],
                                                ALU.mult).then_inc(hc_done, 1)

        @block.scalar
        def _(act):
            def root(b):
                act.wait_ge(dve_ln, LN_STEPS * b + LN_STEPS)
                nc.scalar.activation(rstd[:], rstd[:], ACT.Ln).then_inc(log_ready, 1)
                act.wait_ge(log_ready, b + 1)
                nc.scalar.activation(rstd[:], rstd[:], ACT.Exp, scale=-0.5).then_inc(rstd_ready, 1)

            def row(b, last):
                def emptied(j, out, func, **kw):
                    act.wait_ge(proj_done, JOBS * b + j + 1)
                    nc.scalar.activation(out, ps[0:out.shape[0], j % 8, :], func, **kw).then_inc(evac_done, 1)

                def halves(j, out, func, **kw):
                    for h in range(H):
                        emptied(j + h, out[:, h * BANK:(h + 1) * BANK], func, **kw)

                act.wait_ge(yacc_done, HC + STEPS * b)
                act.wait_ge(scan_done, AGO + STEPS * b)
                for c in range(KD):
                    halves(H * c, xnT[:, c, :], ACT.Copy)
                for e in range(KE):
                    halves(J_IN + H * e, xp[:, e, KC - 1:], ACT.Copy)
                act.wait_ge(gated, ONE + KE * b)
                for e in range(KE):
                    halves(J_IN + H * (KE + e), silu_z[:, e, :], ACT.Silu)
                    for e2 in ((0, 1), (2,), (3,), ())[e]:
                        act.wait_ge(conv_done, KE * b + e2 + 1)
                        nc.scalar.activation(xc[:, e2, :], xc[:, e2, :], ACT.Silu).then_inc(silu_done, 1)
                nc.scalar.preload_act_table_set(EXP_LN)
                halves(J_X, xd_rows, ACT.Copy)

                def rounded(i):
                    if i == 0:
                        act.wait_ge(evac_done, JOBS * b + J_X + H)
                        act.wait_ge(bcast_done, STEPS * b + ONE)
                    else:
                        act.wait_ge(b_sub, 2 * b + i)
                    k = (3 - i) * N
                    src = xd_rows if i == 0 else b_res
                    nc.scalar.activation(b_split[0:k, :], src[0:k, :], ACT.Copy).then_inc(b_rounded, 1)

                def dt(e):
                    halves(J_DT + H * e, delta[:, e, :], ACT.Identity, bias=b_dt[:, e:e + 1])

                def exp_ln(e):
                    act.wait_ge(neg_abs, KE * b + e + 1)
                    nc.scalar.activation(u[:, e, :], u[:, e, :], ACT.Exp).then_inc(exp1_done, 1)
                    act.wait_ge(exp1_done, KE * b + e + 1)
                    nc.scalar.activation(u[:, e, :], u[:, e, :], ACT.Ln, bias=1.0).then_inc(ln_done, 1)

                rounded(0)
                dt(0)
                dt(1)
                rounded(1)
                exp_ln(0)
                dt(2)
                exp_ln(1)
                rounded(2)
                dt(3)
                exp_ln(2)
                exp_ln(3)
                with act.Fori(0, KE) as e:
                    for n in range(N):
                        s = b * STEPS + e * N + n
                        if n == 0:
                            act.wait_ge(delta_done, KE * b + 1 + e)
                        act.wait_ge(scan_done, AGO - AH + 1 + s)
                        nc.scalar.activation(a_ring[n % AH], delta[:, e, :], ACT.Exp,
                                             scale=negA[:, e, n:n + 1]).then_inc(a_ready, 1)
                if not last:
                    root(b + 1)

            nc.scalar.preload_act_table_set(EXP_LN)
            root(0)
            act.wait_ge(consts, 16 * OTHERS)
            nc.scalar.activation(negA[:], negA[:], ACT.Exp).then_inc(negA_ready, 1)
            act.wait_ge(negA_ready, 1)
            nc.scalar.activation(negA[:], negA[:], ACT.Copy, scale=-1.0).then_inc(negA_ready, 1)
            act.wait_ge(sel_ready, 1)
            with act.Fori(0, NB - 1) as b:
                row(b, False)
            row(NB - 1, True)

        @block.vector
        def _(dve):
            def ln_stats(b):
                dve.wait_ge(x_loaded, 16 * b + 16)
                for i in range(NT):
                    nc.vector.bn_stats(stats[:, i, :], xn[:, i, :]).then_inc(dve_ln, 1)
                for i in range(NT):
                    hold(dve, dve_ln, LN_STEPS * b + i + 1)
                    nc.vector.bn_aggr(mv[:, i, :], stats[:, i, :]).then_inc(dve_ln, 1)
                dve.wait_ge(dve_ln, LN_STEPS * b + 2 * NT)
                nc.vector.tensor_scalar(rstd[:], mv[:, :, 1], EPS, None, ALU.add).then_inc(dve_ln, 1)

            def ln_apply(b):
                dve.wait_ge(rstd_ready, b + 1)
                for i in range(NT):
                    nc.vector.tensor_scalar(xn[:, i, :], xn[:, i, :], mv[:, i, 0:1], rstd[:, i:i + 1],
                                            ALU.subtract, ALU.mult).then_inc(xn_ready, 1)

            def finish_y(b, e):
                def read():
                    dve.wait_ge(yacc_done, HC + b * STEPS + e * N + N)
                    nc.vector.scalar_tensor_tensor(out=u[:, e, :], in0=xc[:, e, :], scalar=dvec[:, bass.ds(e, 1)],
                                                   in1=pair_of_banks(Y_PAIR), op0=ALU.mult,
                                                   op1=ALU.add).then_inc(y_read, 1)
                def gate():
                    dve.wait_ge(y_read, ONE + b * KE + e + 1)
                    nc.vector.tensor_tensor(u[:, e, :], u[:, e, :], silu_z[:, e, :], ALU.mult).then_inc(gated, 1)
                return read, gate

            def row(b, last):
                dve.wait_ge(pads, 1 + b)
                for e in range(KE):
                    dve.wait_ge(evac_done, JOBS * b + J_IN + H * (e + 1))
                    nc.vector.tensor_scalar(xc[:, e, :], xp[:, e, 0:T], wconv[:, e, 0:1], None,
                                            ALU.mult).then_inc(conv_step, 1)
                    for k in range(1, KC):
                        dve.wait_ge(conv_step, (KC - 1) * KE * b + (KC - 1) * e + k)
                        nc.vector.scalar_tensor_tensor(
                            out=xc[:, e, :], in0=xp[:, e, k:k + T], scalar=wconv[:, e, k:k + 1], in1=xc[:, e, :],
                            op0=ALU.mult, op1=ALU.add).then_inc(conv_done if k == KC - 1 else conv_step, 1)

                def minus_abs(e):
                    dve.wait_ge(evac_done, JOBS * b + J_DT + H * (e + 1))
                    nc.vector.scalar_tensor_tensor(out=u[:, e, :], in0=delta[:, e, :], scalar=-1.0,
                                                   in1=delta[:, e, :], op0=ALU.mult, op1=ALU.min).then_inc(neg_abs, 1)

                def delta_u(e):
                    dve.wait_ge(ln_done, KE * b + e + 1)
                    nc.vector.scalar_tensor_tensor(out=delta[:, e, :], in0=delta[:, e, :], scalar=0.0,
                                                   in1=u[:, e, :], op0=ALU.max, op1=ALU.add).then_inc(delta_done, 1)
                    dve.wait_ge(delta_done, KE * b + e + 1)
                    dve.wait_ge(silu_done, KE * b + e + 1)
                    nc.vector.tensor_tensor(u[:, e, :], delta[:, e, :], xc[:, e, :], ALU.mult).then_inc(u_done, 1)

                minus_abs(0)
                minus_abs(1)
                minus_abs(2)
                delta_u(0)
                delta_u(1)
                minus_abs(3)
                delta_u(2)
                delta_u(3)

                def bx(e, n):
                    dve.wait_ge(bcast_done, ONE + 1 + b * STEPS + e * N + n)
                    pb = pair_of_banks(B_PAIR[n])
                    nc.vector.tensor_tensor(pb, u[:, e, :], pb, ALU.mult).then_inc(bx_done, 1)

                def steps(e, first):
                    read, gate = (None, None) if first else finish_y(b, e - 1)
                    bx(e, 0)
                    for n in range(N):
                        s = b * STEPS + e * N + n
                        if n + 1 < N:
                            bx(e, n + 1)
                        dve.wait_ge(bx_done, 1 + s)
                        dve.wait_ge(a_ready, 1 + s)
                        dve.wait_ge(hc_done, 1 + s)
                        nc.vector.tensor_tensor_scan(h_ring[n % AH], a_ring[n % AH], pair_of_banks(B_PAIR[n]), 0.0,
                                                     ALU.mult, ALU.add).then_inc(scan_done, 1)
                        if n == 2 and not first:
                            read()
                        if n == 3 and not first:
                            gate()

                dve.wait_ge(u_done, KE * b + KE)
                steps(0, True)
                with dve.Fori(1, KE) as e:
                    steps(e, False)
                if not last:
                    ln_stats(b + 1)
                read, gate = finish_y(b, KE - 1)
                read()
                gate()
                if not last:
                    ln_apply(b + 1)
                dve.wait_ge(res_loaded, 16 * b + 16)
                for i in range(NT):
                    dve.wait_ge(out_done, NT * b + i + 1)
                    nc.vector.tensor_tensor(x_res[:, i, :], ps[:, 4 + i % 4, 0:DM], x_res[:, i, :],
                                            ALU.add).then_inc(res_done, 1)

            nc.vector.sem_inc(scan_done, AGO)
            ln_stats(0)
            ln_apply(0)
            dve.wait_ge(consts, 16 * OTHERS)
            with dve.Fori(0, NB - 1) as b:
                row(b, False)
            row(NB - 1, True)

        @block.tensor
        def _(pe):
            def row(b):
                def bank_free(j):
                    if j >= 8:
                        pe.wait_ge(evac_done, JOBS * b + j - 7)

                for c in range(KD):
                    for h in range(H):
                        j = H * c + h
                        for i in range(4):
                            if c == 0:
                                pe.wait_ge(xn_ready, NT * b + 4 * h + i + 1)
                            last = nc.tensor.transpose(ps[:, j, i * P:(i + 1) * P],
                                                       xn[:, 4 * h + i, c * P:(c + 1) * P], ident[:])
                        last.then_inc(proj_done, 1)
                pe.wait_ge(res_done, ONE + NT * b)
                pe.wait_ge(evac_done, JOBS * b + J_IN)
                for e in range(2 * KE):
                    for h in range(H):
                        j = J_IN + H * e + h
                        bank_free(j)
                        for c in range(KD):
                            last = nc.tensor.matmul(ps[:, j % 8, :], w_in[:, c, e * P:(e + 1) * P],
                                                    xnT[:, c, h * BANK:(h + 1) * BANK],
                                                    start=(c == 0), stop=(c == KD - 1))
                        last.then_inc(proj_done, 1)
                for h in range(H):
                    bank_free(J_X + h)
                    for c in range(KE):
                        if h == 0:
                            pe.wait_ge(silu_done, KE * b + c + 1)
                        last = nc.tensor.matmul(ps[:, (J_X + h) % 8, :], w_x[:, c, :],
                                                xc[:, c, h * BANK:(h + 1) * BANK],
                                                start=(c == 0), stop=(c == KE - 1))
                    last.then_inc(proj_done, 1)
                pe.wait_ge(evac_done, JOBS * b + J_X + H)
                for e in range(KE):
                    for h in range(H):
                        j = J_DT + H * e + h
                        bank_free(j)
                        nc.tensor.matmul(ps[:, j % 8, :], w_dt[DT0:DT0 + R, e * P:(e + 1) * P],
                                         xd_rows[DT0:DT0 + R, h * BANK:(h + 1) * BANK],
                                         start=True, stop=True).then_inc(proj_done, 1)
                pe.wait_ge(b_rounded, 3 * b + 3)
                pe.wait_ge(evac_done, JOBS * b + JOBS)

                def bcast(e, n):
                    s = b * STEPS + e * N + n
                    pe.wait_ge(scan_done, AGO + 1 + s - B_AGO[n])
                    for h in range(H):
                        last = nc.tensor.matmul(ps[:, 2 * B_PAIR[n] + h, :], sel[:, n, :],
                                                b_split[:, h * BANK:(h + 1) * BANK], start=True, stop=True)
                    last.then_inc(bcast_done, 1)

                def yacc(e, n):
                    pe.wait_ge(hc_done, AH + 1 + b * STEPS + e * N + n)
                    if n == 0:
                        pe.wait_ge(y_read, ONE + b * KE + e)
                    for h in range(H):
                        last = nc.tensor.matmul(ps[:, 2 * Y_PAIR + h, :], ident[:],
                                                hc_ring[n % HC][:, h * BANK:(h + 1) * BANK],
                                                start=(n == 0), stop=(n == N - 1))
                    last.then_inc(yacc_done, 1)

                for n in range(N):
                    bcast(0, n)
                    if n >= LAG:
                        yacc(0, n - LAG)
                with pe.Fori(1, KE) as e:
                    for n in range(N):
                        bcast(e, n)
                        if n < LAG:
                            yacc(e - 1, n - LAG + N)
                        else:
                            yacc(e, n - LAG)
                for n in range(N - LAG, N):
                    yacc(KE - 1, n)
                pe.wait_ge(gated, ONE + KE * b + KE)
                for i in range(NT):
                    if i >= 4:
                        pe.wait_ge(res_done, ONE + NT * b + i - 3)
                    for c in range(KE):
                        last = nc.tensor.matmul(ps[:, 4 + i % 4, 0:DM], u[:, c, i * P:(i + 1) * P], w_out[:, c, :],
                                                start=(c == 0), stop=(c == KE - 1))
                    last.then_inc(out_done, 1)

            pe.sem_inc(bcast_done, ONE)
            nc.tensor.sem_inc(yacc_done, HC)
            pe.wait_ge(w_in_loaded, 16 * 2)
            pe.wait_ge(consts, 16 * OTHERS)
            pe.wait_ge(sel_ready, 1)
            with pe.Fori(0, NB) as b:
                row(b)


def attention_phase(nc, x1, ctx_t, pos, wq, wk, wv, wo, bq, bk, bv, bo, ident_c, head_mask_c, v_mask_c, inv_freq_c, gate_w,
                    x2, xn2, logits):
    NBR, T, DM = x1.shape
    M = ctx_t.shape[1] // NBR
    NH, HD, E = 16, 16, gate_w.shape[1]
    HP = NH // 2
    KD = DM // P
    CH = BANK
    TI = CH // P
    NC = NBR * T // CH
    CB = T // CH
    HM = HP // 2 * M
    SCALE = HD ** -0.5
    G = v_mask_c.shape[1]
    ROWS = [min(P, HP * M - g * P) for g in range(G)]
    NU = 2 * G
    REP = 3
    assert (G - 1) * P % M + P <= REP * M and M - 1 + P <= REP * M
    TWO_PI = 2 * np.pi
    C1 = 6.28125
    C2 = float(np.float32(np.floor((TWO_PI - C1) * 2 ** 20) / 2 ** 20))
    C3 = TWO_PI - C1 - C2
    ROUND = 1.5 * 2 ** 23
    PI_IN = 3.1415925

    x1c = x1.rearrange("b (c i p) d -> (b c) p i d", p=P, i=TI)
    xn2c = xn2.rearrange("(c i p) d -> c p i d", i=TI, p=P)
    x2c = x2.rearrange("b (c i p) d -> (b c) p i d", p=P, i=TI)

    with ExitStack() as ctx:
        def sb(name, shape, dt=F32):
            return ctx.enter_context(nc.sbuf_tensor(name, shape, dt))

        def sem(name):
            return ctx.enter_context(nc.semaphore(name))

        ident = sb("t_ident", [P, P])
        wq_sb, wk_sb, wv_sb, wo_sb = (sb(f"t_{n}", [P, KD, DM]) for n in ("wq", "wk", "wv", "wo"))
        gw_sb = sb("t_gw", [P, KD, E])
        bq_bc, bv_bc, bo_bc = (sb(f"t_{n}", [P, DM]) for n in ("bq", "bv", "bo"))
        bk_col = sb("t_bk", [P, KD])
        mask = sb("t_mask", [P, HP])
        inv_freq = sb("t_inv_freq", [P, HD // 2])
        k_blk = sb("t_k_blk", [P, KD, NBR, HP * M])
        ctx_rep = sb("t_ctx_rep", [P, KD, NBR, REP * M])
        v_all = sb("t_v_all", [P, NBR, G, DM])
        v_mask = sb("t_v_mask", [P, G, HP])
        v_cur = sb("t_v_cur", [P, G, DM])
        pos_i = sb("t_pos_i", [P, NC * TI], I32)
        pos_f = sb("t_pos_f", [P, NC * TI])
        trig = [sb(f"t_trig{i}", [P, NC * TI, HD // 2]) for i in range(5)]
        ang, turns, sin_t, cos_t, tmp_t = trig
        xa = sb("t_xa", [P, NC, TI, DM])
        stats = sb("t_stats", [P, TI, 6])
        mv1, mv2 = sb("t_mv1", [P, TI, 2]), sb("t_mv2", [P, TI, 2])
        rstd1, rstd2 = sb("t_rstd1", [P, TI]), sb("t_rstd2", [P, TI])
        stats2 = sb("t_stats2", [P, TI, 6])
        xn = sb("t_xn", [P, TI, DM])
        xnT = sb("t_xnT", [P, KD, CH])
        q = sb("t_q", [P, TI, DM])
        q_rot = sb("t_q_rot", [P, TI, DM])
        rope_a = sb("t_rope_a", [P, TI, NH, HD // 2])
        rope_b = sb("t_rope_b", [P, TI, NH, HD // 2])
        qT = sb("t_qT", [P, 2, KD, CH])
        probs = sb("t_probs", [P, 2, TI, NH * M])
        early = probs[:, 0, :, :].rearrange("p i (c n) -> p i c n", c=2)
        kT = early[:, 1, :, 0:NBR * M]
        mx = sb("t_mx", [P, 2, HP])
        total = sb("t_total", [P, 2, HP])
        rtotal = sb("t_rtotal", [P, 4, HP])
        pT = sb("t_pT", [P, G, CH])
        oT = sb("t_oT", [P, 2, KD, CH])
        xn2s = sb("t_xn2s", [P, TI, DM])
        xn2T = sb("t_xn2T", [P, KD, CH])
        ps = ctx.enter_context(nc.psum_tensor("t_ps", [P, 8, BANK], F32))
        S_BANK, T_BANK, O_BANK, JOB_BANK = 0, 4, 6, 7

        angle_consts, k_consts, consts = sem("t_angle_consts"), sem("t_k_consts"), sem("t_consts")
        held = sem("t_held")
        k_done, k_evac, k_blocks = sem("t_k_done"), sem("t_k_evac"), sem("t_k_blocks")
        v_done, v_evac, v_copied = sem("t_v_done"), sem("t_v_evac"), sem("t_v_copied")
        trig_step, sin_done = sem("t_trig_step"), sem("t_sin_done")
        x_loaded = sem("t_x_loaded")
        ln1, rstd1_ready, xn_ready = sem("t_ln1"), sem("t_rstd1_ready"), sem("t_xn_ready")
        a_job, a_evac = sem("t_a_job"), sem("t_a_evac")
        d_job, d_evac = sem("t_d_job"), sem("t_d_evac")
        rope_step = sem("t_rope_step")
        s_done, mx_done, sub_done, exp_done = sem("t_s_done"), sem("t_mx_done"), sem("t_sub_done"), sem("t_exp_done")
        sum_done, rs_done, norm_done = sem("t_sum_done"), sem("t_rs_done"), sem("t_norm_done")
        tr_done, tr_evac, pv_done, o_evac = sem("t_tr_done"), sem("t_tr_evac"), sem("t_pv_done"), sem("t_o_evac")
        bo_added = sem("t_bo_added")
        log1_done, log2_done = sem("t_log1_done"), sem("t_log2_done")
        ln2, rstd2_ready, xn2_ready = sem("t_ln2"), sem("t_rstd2_ready"), sem("t_xn2_ready")
        x2_stored, xn2_kept = sem("t_x2_stored"), sem("t_xn2_kept")
        V_FILLS = NBR * G // 2
        N_ANGLE, N_K, N_CONST = 16 * 2, 16 * (3 + REP * KD), 16 * 9
        AJ, DJ, HT = 6, 5, 2 * TI
        LN = 2 * TI + 1

        def hold(eng, of, value):
            eng.wait_ge(of, value)
            eng.sem_inc(held, 1)

        JOBS = [[("A", 0), ("A", 1)], [("A", 2), ("D", 0)], [("A", 3), ("D", 1)], [], [("D", 2)], [("D", 3)],
                [("D", 4), ("A", 4)], [("A", 5)]]

        def jobs_of(has_a, has_d):
            return [[j for j in slot if (has_a if j[0] == "A" else has_d)] for slot in JOBS]

        def units(j):
            return range(NU * j // HT, NU * (j + 1) // HT)

        def c_par(k):
            return k % 2

        def run(eng, iteration):
            def one(it, static=None):
                k = it if static is None else static
                iteration(it, k, 0 <= k + 3 < NC, 0 <= k + 2 < NC, 0 <= k + 1 < NC, 0 <= k < NC, 0 <= k - 1 < NC)
            for it in range(-3, 1):
                one(it)
            loops = (NC - 4) // 2
            with eng.Fori(0, loops) as i:
                one(1 + 2 * i, 1)
                one(2 + 2 * i, 2)
            for it in range(1 + 2 * loops, NC + 1):
                one(it)

        block = ctx.enter_context(nc.Block())

        ONE = 1

        @block.sync
        def _(sp):
            sp.sem_inc(xn2_kept, ONE)
            sp.dma_start(xa[:, 0, :, :], x1c[0]).then_inc(x_loaded, 16)
            for loaded, pairs in (
                    (angle_consts, [(pos_i[:], pos), (inv_freq[:], inv_freq_c)]),
                    (k_consts, [(ctx_rep[:, c, :, r * M:(r + 1) * M],
                                 ctx_t[c * P:(c + 1) * P, :].rearrange("p (b m) -> p b m", m=M))
                                for c in range(KD) for r in range(REP)] +
                     [(wk_sb[:], wk.rearrange("(c p) e -> p c e", p=P)), (bk_col[:], bk), (mask[:], head_mask_c)]),
                    (consts, [(ident[:], ident_c), (wq_sb[:], wq.rearrange("(c p) e -> p c e", p=P)),
                              (bq_bc[:], bq.unsqueeze(0).to_broadcast([P, DM])),
                              (wv_sb[:], wv.rearrange("(c p) e -> p c e", p=P)),
                              (bv_bc[:], bv.unsqueeze(0).to_broadcast([P, DM])), (v_mask[:], v_mask_c),
                              (wo_sb[:], wo.rearrange("(c p) e -> p c e", p=P)),
                              (gw_sb[:], gate_w.rearrange("(c p) e -> p c e", p=P)),
                              (bo_bc[:], bo.unsqueeze(0).to_broadcast([P, DM]))])):
                for dst, src in pairs:
                    sp.dma_start(dst, src).then_inc(loaded, 16)

            def load(c):
                sp.dma_start(xa[:, c, :, :], x1c[c]).then_inc(x_loaded, 16)

            def iteration(it, k, has_l, has_a, has_b, has_c, has_d):
                if has_l:
                    if k + 3 > 0:
                        sp.wait_ge(x_loaded, 16 * (it + 3))
                        load(it + 3)
                if has_d:
                    c = it - 1
                    sp.wait_ge(d_evac, DJ * c + 2)
                    sp.dma_start(x2c[c], xa[:, c, :, :]).then_inc(x2_stored, 16)
                    sp.wait_ge(xn2_ready, TI * c + TI)
                    sp.dma_start(xn2c[c], xn2s[:]).then_inc(xn2_kept, 16)
            run(sp, iteration)
            sp.wait_ge(x2_stored, 16 * NC)
            sp.wait_ge(xn2_kept, ONE + 16 * NC)

        @block.gpsimd
        def _(pool):
            def iteration(it, k, has_l, has_a, has_b, has_c, has_d):
                if has_c and k % CB == 0:
                    b = it // CB
                    pool.wait_ge(consts, N_CONST)
                    pool.wait_ge(v_evac, V_FILLS)
                    hold(pool, pv_done, NU * it)
                    for g in range(G):
                        nc.gpsimd.tensor_tensor(
                            v_cur[:, g, :].rearrange("p (a h d) -> p a h d", a=2, d=HD),
                            v_all[:, b, g, :].rearrange("p (a h d) -> p a h d", a=2, d=HD),
                            v_mask[:, g, :].unsqueeze(1).unsqueeze(3).to_broadcast([P, 2, HP, HD]),
                            ALU.mult).then_inc(v_copied, 1)

                def normalise(c, j):
                    hold(pool, rs_done, HT * c + j + 1)
                    v = probs[:, c_par(k + 1), j // 2, (j % 2) * HP * M:(j % 2 + 1) * HP * M] \
                        .rearrange("p (h m) -> p h m", m=M)
                    nc.gpsimd.tensor_tensor(v, v, rtotal[:, j % 4, :].unsqueeze(2).to_broadcast([P, HP, M]),
                                            ALU.mult).then_inc(norm_done, 1)

                def rope(c):
                    def half(t, n):
                        return t[:].rearrange("p i (h d) -> p i h d", d=HD)[:, :, :, n * HD // 2:(n + 1) * HD // 2]

                    def table(t):
                        return t[:, bass.ds(c * TI, TI), :].unsqueeze(2).to_broadcast([P, TI, NH, HD // 2])

                    n = 6 * c
                    pool.wait_ge(sin_done, 2)
                    hold(pool, a_evac, AJ * c + 4)
                    tt = nc.gpsimd.tensor_tensor
                    tt(rope_a[:], half(q, 0), table(cos_t), ALU.mult).then_inc(rope_step, 1)
                    hold(pool, rope_step, n + 1)
                    tt(rope_b[:], half(q, 1), table(sin_t), ALU.mult).then_inc(rope_step, 1)
                    hold(pool, rope_step, n + 2)
                    hold(pool, a_job, AJ * c)
                    tt(half(q_rot, 0), rope_a[:], rope_b[:], ALU.subtract).then_inc(rope_step, 1)
                    hold(pool, rope_step, n + 3)
                    tt(rope_a[:], half(q, 1), table(cos_t), ALU.mult).then_inc(rope_step, 1)
                    hold(pool, rope_step, n + 4)
                    tt(rope_b[:], half(q, 0), table(sin_t), ALU.mult).then_inc(rope_step, 1)
                    hold(pool, rope_step, n + 5)
                    tt(half(q_rot, 1), rope_a[:], rope_b[:], ALU.add).then_inc(rope_step, 1)

                if has_a:
                    rope(it + 2)
                if has_b:
                    for j in range(HT):
                        normalise(it + 1, j)
                if has_c:
                    hold(pool, ln1, LN * it + LN)
                    hold(pool, xn_ready, TI * it + TI)
                    v = xa[:, it, :, :]
                    nc.gpsimd.tensor_tensor(v, v, bo_bc[:].unsqueeze(1).to_broadcast([P, TI, DM]),
                                            ALU.add).then_inc(bo_added, 1)
            run(pool, iteration)

        @block.scalar
        def _(act):
            act.wait_ge(k_consts, N_K)
            for c in range(KD):
                act.wait_ge(k_done, c + 1)
                nc.scalar.activation(kT[:, c, :], ps[:, c, 0:NBR * M], ACT.Identity,
                                     bias=bk_col[:, c:c + 1]).then_inc(k_evac, 1)
            act.wait_ge(trig_step, 8)
            nc.scalar.activation(sin_t[:], ang[:], ACT.Sin).then_inc(sin_done, 1)
            act.wait_ge(trig_step, 10)
            nc.scalar.activation(cos_t[:], tmp_t[:], ACT.Sin).then_inc(sin_done, 1)
            nc.scalar.preload_act_table_set(EXP_LN)

            def iteration(it, k, has_l, has_a, has_b, has_c, has_d):
                jobs = jobs_of(has_a, has_d)

                def root(rstd, log_done, c, ready):
                    nc.scalar.activation(rstd[:], rstd[:], ACT.Ln).then_inc(log_done, 1)
                    act.wait_ge(log_done, c + 1)
                    nc.scalar.activation(rstd[:], rstd[:], ACT.Exp, scale=-0.5).then_inc(ready, 1)

                def exps(j):
                    c = it + 1
                    act.wait_ge(sub_done, HT * c + j + 1)
                    v = probs[:, c_par(k + 1), j // 2, (j % 2) * HP * M:(j % 2 + 1) * HP * M]
                    nc.scalar.activation(v, v, ACT.Exp, scale=SCALE).then_inc(exp_done, 1)

                def heads(u):
                    act.wait_ge(tr_done, NU * it + u + 1)
                    if not (k == 0 and u < G):
                        act.wait_ge(pv_done, NU * it + u - G + 1)
                    n = ROWS[u % G]
                    nc.scalar.activation(pT[0:n, u % G, :], ps[0:n, T_BANK + u % 2, :], ACT.Copy).then_inc(tr_evac, 1)
                    if u == G + 1:
                        half_out(0)

                def half_out(hf):
                    act.wait_ge(pv_done, NU * it + (hf + 1) * G)
                    nc.scalar.activation(oT[:, c_par(k), hf, :], ps[:, O_BANK, :], ACT.Copy).then_inc(o_evac, 1)

                for j in range(HT):
                    if has_c:
                        for u in units(j):
                            heads(u)
                    if has_b and j:
                        exps(j - 1)
                    for kind, n in jobs[j]:
                        if kind == "A" and n in (0, 1, 4, 5):
                            act.wait_ge(a_job, AJ * (it + 2) + n + 1)
                            dst = xnT[:, n, :] if n < 2 else qT[:, c_par(k), n - 4, :]
                            nc.scalar.activation(dst, ps[:, JOB_BANK, :], ACT.Copy).then_inc(a_evac, 1)
                        elif kind == "D" and n in (2, 3):
                            act.wait_ge(d_job, DJ * (it - 1) + n + 1)
                            nc.scalar.activation(xn2T[:, n - 2, :], ps[:, JOB_BANK, :], ACT.Copy).then_inc(d_evac, 1)
                    if j == 2 and has_d:
                        act.wait_ge(ln2, LN * (it - 1) + LN)
                        root(rstd2, log2_done, it - 1, rstd2_ready)
                    if j == HT - 2 and has_l:
                        act.wait_ge(ln1, LN * (it + 3) + LN)
                        root(rstd1, log1_done, it + 3, rstd1_ready)
                if has_b:
                    exps(HT - 1)
                if has_c:
                    half_out(1)
            run(act, iteration)

        @block.vector
        def _(dve):
            dve.wait_ge(angle_consts, N_ANGLE)
            def step(ins, n):
                ins.then_inc(trig_step, 1)
                dve.wait_ge(trig_step, n)

            v = nc.vector
            step(v.tensor_copy(pos_f[:], pos_i[:]), 1)
            step(v.tensor_tensor(ang[:], pos_f[:].unsqueeze(2).to_broadcast([P, NC * TI, HD // 2]),
                                 inv_freq[:].unsqueeze(1).to_broadcast([P, NC * TI, HD // 2]), ALU.mult), 2)
            step(v.tensor_scalar(turns[:], ang[:], 1 / TWO_PI, ROUND, ALU.mult, ALU.add), 3)
            step(v.tensor_scalar(turns[:], turns[:], ROUND, None, ALU.subtract), 4)
            for n, part in enumerate((C1, C2, C3)):
                step(v.scalar_tensor_tensor(out=ang[:], in0=turns[:], scalar=-part, in1=ang[:],
                                            op0=ALU.mult, op1=ALU.add), 5 + n)
            step(v.tensor_scalar(ang[:], ang[:], PI_IN, -PI_IN, ALU.min, ALU.max), 8)
            step(v.scalar_tensor_tensor(out=tmp_t[:], in0=ang[:], scalar=-1.0, in1=ang[:],
                                        op0=ALU.mult, op1=ALU.min), 9)
            step(v.tensor_scalar(tmp_t[:], tmp_t[:], np.pi / 2, None, ALU.add), 10)
            dve.wait_ge(k_consts, N_K)
            for c in range(KD):
                dve.wait_ge(k_evac, c + 1)
                for h in range(HP):
                    v.tensor_scalar(k_blk[:, c, :, h * M:(h + 1) * M], kT[:, c, :].rearrange("p (b m) -> p b m", m=M),
                                    mask[:, h:h + 1], None, ALU.mult).then_inc(k_blocks, 1)
            dve.wait_ge(k_blocks, KD * HP)
            dve.wait_ge(consts, N_CONST)

            def values():
                for f in range(V_FILLS):
                    dve.wait_ge(v_done, f + 1)
                    v.tensor_tensor(v_all[:].rearrange("p b g d -> p (b g) d")[:, 2 * f:2 * f + 2, :],
                                    ps[:, f % 4, :].rearrange("p (i d) -> p i d", d=DM),
                                    bv_bc[:].unsqueeze(1).to_broadcast([P, 2, DM]), ALU.add).then_inc(v_evac, 1)

            def norm(c, xin, st, mv, rstd, chain, rstd_ready, out, ready):
                def first():
                    for i in range(TI):
                        v.bn_stats(st[:, i, :], xin(i)).then_inc(chain, 1)
                    for i in range(TI):
                        hold(dve, chain, LN * c + i + 1)
                        v.bn_aggr(mv[:, i, :], st[:, i, :]).then_inc(chain, 1)
                    dve.wait_ge(chain, LN * c + 2 * TI)
                    v.tensor_scalar(rstd[:], mv[:, :, 1], EPS, None, ALU.add).then_inc(chain, 1)

                def second():
                    dve.wait_ge(chain, LN * c + 2 * TI)
                    dve.wait_ge(rstd_ready, c + 1)
                    for i in range(TI):
                        v.tensor_scalar(out(i), xin(i), mv[:, i, 0:1], rstd[:, i:i + 1],
                                        ALU.subtract, ALU.mult).then_inc(ready, 1)
                return first, second

            def iteration(it, k, has_l, has_a, has_b, has_c, has_d):
                jobs = jobs_of(has_a, has_d)
                if has_d:
                    d = it - 1
                    ln2_first, ln2_second = norm(d, lambda i: xa[:, d, i, :], stats2, mv2, rstd2, ln2, rstd2_ready,
                                                 lambda i: xn2s[:, i, :], xn2_ready)
                if has_l:
                    ln1_first, ln1_second = norm(it + 3, lambda i: xa[:, it + 3, i, :], stats, mv1, rstd1, ln1,
                                                 rstd1_ready, lambda i: xn[:, i, :], xn_ready)

                def scores(j):
                    c, par = it + 1, c_par(k + 1)
                    s = ps[:, S_BANK + 2 * (j % 2):S_BANK + 2 * (j % 2) + 2, 0:HM].rearrange("p a (h m) -> p a h m", m=M)
                    m2 = mx[:, j % 2, :].rearrange("p (a h) -> p a h", a=2)
                    out = probs[:, par, j // 2, (j % 2) * HP * M:(j % 2 + 1) * HP * M] \
                        .rearrange("p (a h m) -> p a h m", a=2, m=M)
                    dve.wait_ge(s_done, HT * c + j + 1)
                    v.reduce_max(m2, s, AXX).then_inc(mx_done, 1)
                    if k + 1 >= 2:
                        dve.wait_ge(tr_done, NU * (c - 1))
                    dve.wait_ge(mx_done, HT * c + j + 1)
                    v.tensor_tensor(out, s, m2.unsqueeze(3).to_broadcast([P, 2, HP // 2, M]),
                                    ALU.subtract).then_inc(sub_done, 1)

                def sums(j):
                    c, par = it + 1, c_par(k + 1)
                    src = probs[:, par, j // 2, (j % 2) * HP * M:(j % 2 + 1) * HP * M].rearrange("p (h m) -> p h m", m=M)
                    dve.wait_ge(exp_done, HT * c + j + 1)
                    v.reduce_sum(total[:, j % 2, :], src, AXX).then_inc(sum_done, 1)
                    if not (k + 1 == 0 and j < 4):
                        dve.wait_ge(norm_done, HT * c + j - 3)
                    dve.wait_ge(sum_done, HT * c + j + 1)
                    v.reciprocal(rtotal[:, j % 4, :], total[:, j % 2, :]).then_inc(rs_done, 1)

                if k == -2:
                    values()
                for j in range(HT):
                    if has_b:
                        scores(j)
                        if j > 1:
                            sums(j - 2)
                    for kind, n in jobs[j]:
                        if kind == "A" and n in (2, 3):
                            c = it + 2
                            dve.wait_ge(a_job, AJ * c + n + 1)
                            if k + 2 > 0:
                                dve.wait_ge(rope_step, 6 * c)
                            v.tensor_tensor(q[:, 2 * (n - 2):2 * (n - 2) + 2, :],
                                            ps[:, JOB_BANK, :].rearrange("p (i d) -> p i d", d=DM),
                                            bq_bc[:].unsqueeze(1).to_broadcast([P, 2, DM]),
                                            ALU.add).then_inc(a_evac, 1)
                        elif kind == "D" and n in (0, 1):
                            dve.wait_ge(d_job, DJ * d + n + 1)
                            dve.wait_ge(bo_added, d + 1)
                            xv = xa[:, d, 2 * n:2 * n + 2, :]
                            v.tensor_tensor(xv, ps[:, JOB_BANK, :].rearrange("p (i d) -> p i d", d=DM), xv,
                                            ALU.add).then_inc(d_evac, 1)
                        elif kind == "D" and n == 4:
                            dve.wait_ge(d_job, DJ * d + n + 1)
                            v.tensor_copy(logits[:, bass.ds(d * TI, TI), :],
                                          ps[:, JOB_BANK, 0:TI * E].rearrange("p (i e) -> p i e", e=E)).then_inc(d_evac, 1)
                    if j == 2 and has_d:
                        hold(dve, d_evac, DJ * d + 2)
                        ln2_first()
                    if j == 3 and has_d:
                        dve.wait_ge(xn2_kept, ONE + 16 * d)
                        ln2_second()
                    if j == HT - 2 and has_l:
                        hold(dve, x_loaded, 16 * (it + 4))
                        ln1_first()
                if has_b:
                    sums(HT - 2)
                    sums(HT - 1)
                if has_l:
                    dve.wait_ge(a_job, AJ * (it + 3) - 4 if has_a else 0)
                    ln1_second()
            run(dve, iteration)

        @block.tensor
        def _(pe):
            pe.wait_ge(k_consts, N_K)
            t = nc.tensor
            for c in range(KD):
                for n in range(KD):
                    last = t.matmul(ps[:, c, 0:NBR * M], wk_sb[:, n, c * P:(c + 1) * P], ctx_rep[:, n, :, 0:M],
                                    start=(n == 0), stop=(n == KD - 1))
                last.then_inc(k_done, 1)
            pe.wait_ge(consts, N_CONST)

            def values():
                pe.wait_ge(k_evac, KD)
                for f in range(V_FILLS):
                    if f >= 4:
                        pe.wait_ge(v_evac, f - 3)
                    for i in range(2):
                        b, g = (2 * f + i) // G, (2 * f + i) % G
                        for n in range(KD):
                            last = t.matmul(ps[:, f % 4, i * DM:(i + 1) * DM],
                                            ctx_rep[:, n, b, g * P % M:g * P % M + P], wv_sb[:, n, :],
                                            start=(n == 0), stop=(n == KD - 1))
                    last.then_inc(v_done, 1)

            def iteration(it, k, has_l, has_a, has_b, has_c, has_d):
                jobs = jobs_of(has_a, has_d)
                order = [j for slot in jobs for j in slot]

                def bank_emptied(kind, n):
                    at = order.index((kind, n))
                    if at:
                        before, m = order[at - 1]
                        shift = 0
                    else:
                        was = [j for slot in jobs_of(0 <= k + 1 < NC, 0 <= k - 2 < NC) for j in slot]
                        if not was:
                            return
                        (before, m), shift = was[-1], -1
                    if before == "A":
                        pe.wait_ge(a_evac, AJ * (it + shift + 2) + m + 1)
                    else:
                        pe.wait_ge(d_evac, DJ * (it + shift - 1) + m + 1)

                def job(kind, n):
                    bank_emptied(kind, n)
                    out = ps[:, JOB_BANK, :]
                    if kind == "A":
                        c = it + 2
                        if n in (0, 1):
                            pe.wait_ge(xn_ready, TI * c + TI)
                            if n == 0 and k + 2 > 0:
                                hold(pe, a_job, AJ * c)
                            for i in range(TI):
                                last = t.transpose(out[:, i * P:(i + 1) * P], xn[:, i, n * P:(n + 1) * P], ident[:])
                        elif n in (2, 3):
                            pe.wait_ge(a_evac, AJ * c + 2)
                            for i in range(2):
                                tile = 2 * (n - 2) + i
                                for m in range(KD):
                                    last = t.matmul(out[:, i * DM:(i + 1) * DM], xnT[:, m, tile * P:(tile + 1) * P],
                                                    wq_sb[:, m, :], start=(m == 0), stop=(m == KD - 1))
                        else:
                            pe.wait_ge(rope_step, 6 * c + 6)
                            for i in range(TI):
                                last = t.transpose(out[:, i * P:(i + 1) * P], q_rot[:, i, (n - 4) * P:(n - 3) * P],
                                                   ident[:])
                        last.then_inc(a_job, 1)
                    else:
                        c, par = it - 1, c_par(k - 1)
                        if n in (0, 1):
                            pe.wait_ge(o_evac, 2 * c + 2)
                            for i in range(2):
                                tile = 2 * n + i
                                for m in range(KD):
                                    last = t.matmul(out[:, i * DM:(i + 1) * DM], oT[:, par, m, tile * P:(tile + 1) * P],
                                                    wo_sb[:, m, :], start=(m == 0), stop=(m == KD - 1))
                        elif n in (2, 3):
                            pe.wait_ge(xn2_ready, TI * c + TI)
                            for i in range(TI):
                                last = t.transpose(out[:, i * P:(i + 1) * P],
                                                   xn2s[:, i, (n - 2) * P:(n - 1) * P], ident[:])
                        else:
                            pe.wait_ge(d_evac, DJ * c + 4)
                            for i in range(TI):
                                for m in range(KD):
                                    last = t.matmul(out[:, i * E:(i + 1) * E], xn2T[:, m, i * P:(i + 1) * P],
                                                    gw_sb[:, m, :], start=(m == 0), stop=(m == KD - 1))
                        last.then_inc(d_job, 1)

                def scores(j):
                    c, par = it + 1, c_par(k + 1)
                    b = c // CB
                    if j == 0:
                        pe.wait_ge(a_evac, AJ * c + AJ)
                    if not (k + 1 == 0 and j < 2):
                        pe.wait_ge(sub_done, HT * c + j - 1)
                    i, hf = j // 2, j % 2
                    for a in range(2):
                        last = t.matmul(ps[:, S_BANK + 2 * (j % 2) + a, 0:HM], qT[:, par, hf, i * P:(i + 1) * P],
                                        k_blk[:, hf, b, a * HM:(a + 1) * HM], start=True, stop=True)
                    last.then_inc(s_done, 1)

                def turn(u):
                    pe.wait_ge(norm_done, HT * it + HT - 1 + u // G)
                    if not (k == 0 and u < 2):
                        pe.wait_ge(tr_evac, NU * it + u - 1)
                    n = ROWS[u % G]
                    lo = u // G * HP * M + u % G * P
                    for i in range(TI):
                        last = t.transpose(ps[0:n, T_BANK + u % 2, i * P:(i + 1) * P],
                                           probs[:, c_par(k), i, lo:lo + n], ident[:])
                    last.then_inc(tr_done, 1)

                def times_v(u):
                    pe.wait_ge(tr_evac, NU * it + u + 1)
                    if u == 0:
                        pe.wait_ge(v_copied, G * (it // CB) + G)
                    if u % G == 0 and not (k == 0 and u == 0):
                        pe.wait_ge(o_evac, 2 * it + u // G)
                    g, n = u % G, ROWS[u % G]
                    t.matmul(ps[:, O_BANK, :], v_cur[0:n, g, u // G * P:(u // G + 1) * P], pT[0:n, g, :],
                             start=(g == 0), stop=(g == G - 1)).then_inc(pv_done, 1)

                if k == -2:
                    values()
                if k == -1:
                    pe.wait_ge(v_evac, V_FILLS)
                    pe.wait_ge(k_blocks, KD * HP)
                for j in range(HT):
                    if has_b:
                        scores(j)
                    if has_c:
                        for u in units(j):
                            turn(u)
                            if u >= 2:
                                times_v(u - 2)
                    for kind, n in jobs[j]:
                        job(kind, n)
                if has_c:
                    times_v(NU - 2)
                    times_v(NU - 1)
            run(pe, iteration)


def dispatch_phase(nc, logits, lower_c, token_c, expert_c, iota_c, gate_up_w, down_w, w1, w2, w_loaded,
                   tables, ids, weights, xn2, out):
    NT, E = logits.shape[1], logits.shape[2]
    TILES = tables.shape[2]
    D = out.shape[1]
    NTOK = NT * P
    TT = 4

    with ExitStack() as ctx:
        def sb(name, shape, dt=F32):
            return ctx.enter_context(nc.sbuf_tensor(name, shape, dt))

        def sem(name):
            return ctx.enter_context(nc.semaphore(name))

        lower = sb("d_lower", [P, 2, P])
        token = sb("d_token", [P, NT + 1])
        expert = sb("d_expert", [P, 2, E])
        iota = sb("d_iota", [P, P])
        p = sb("d_p", [P, NT, E])
        p2 = sb("d_p2", [P, NT, E])
        one1, one2 = sb("d_one1", [P, NT, E]), sb("d_one2", [P, NT, E])
        both = sb("d_both", [P, NT, E])
        cand = sb("d_cand", [P, NT, E])
        where = sb("d_where", [P, NT, E])
        upto = sb("d_upto", [P, NT, E])
        ones = sb("d_ones", [P, NT])
        row = {n: sb(f"d_{n}", [P, NT]) for n in ("m", "s", "r", "m1", "i1", "m2", "i2", "den")}
        weight, pos = sb("d_weight", [P, NT, 2]), sb("d_pos", [P, NT, 2])
        pos_i, low_i = sb("d_pos_i", [P, NT, 2], I32), sb("d_low_i", [P, NT, 2], I32)
        tile_of, row_of = sb("d_tile_of", [P, NT, 2]), sb("d_row_of", [P, NT, 2])
        number = sb("d_number", [P, NT, 2])
        is_row = sb("d_is_row", [P, 2, 2 * TT, P])
        is_tile = sb("d_is_tile", [P, 2, 2 * TT, TILES])
        at_tile = sb("d_at_tile", [P, 2, 2 * TT, 2, TILES])
        zero_rows = sb("d_zero_rows", [P, D])
        nt_f, nt_i = sb("d_nt_f", [P, E]), sb("d_nt_i", [P, E], I32)
        tend, tstart = sb("d_tend", [P, E]), sb("d_tstart", [P, E])
        passed = sb("d_passed", [1, TILES, E])
        eid = sb("d_eid", [1, TILES])
        need = sb("d_need", [1, TILES])
        expert_i = sb("d_expert_i", [1, TILES], I32)
        ps = ctx.enter_context(nc.psum_tensor("d_ps", [P, 3, BANK], F32))

        consts, step, shifted, counted = sem("d_consts"), sem("d_step"), sem("d_shifted"), sem("d_counted")
        exp_done, zeroed, blank = sem("d_exp_done"), sem("d_zeroed"), sem("d_blank")
        placed, is_tile_ready = sem("d_placed"), sem("d_is_tile_ready")
        row_ready, number_ready = sem("d_row_ready"), sem("d_number_ready")
        weight_ready, listed = sem("d_weight_ready"), sem("d_listed")
        block = ctx.enter_context(nc.Block())

        def over_e(t):
            return t[:].unsqueeze(2).to_broadcast([P, NT, E])

        def over_t(t):
            return t.unsqueeze(1).to_broadcast([P, NT, E])

        def turns(eng, body):
            n = NT // TT // 2
            for h in range(2):
                body(h, h, True, False)
            with eng.Fori(1, n - 1) as g:
                for h in range(2):
                    body(2 * g + h, h, False, False)
            for h in range(2):
                body(2 * (n - 1) + h, h, False, True)

        def of_turn(v, t):
            return v[:, bass.ds(TT * t, TT), :].rearrange("p i k -> p (i k)")

        def value_at_tile(eng, t, h, a, value):
            return eng.tensor_tensor(at_tile[:, h, :, a, :], is_tile[:, h],
                                     of_turn(value, t).unsqueeze(2).to_broadcast([P, 2 * TT, TILES]), ALU.mult)

        @block.sync
        def _(sp):
            for dst, src in [(lower[:], lower_c), (token[:], token_c), (expert[:], expert_c), (iota[:], iota_c)]:
                sp.dma_start(dst, src).then_inc(consts, 16)
            sp.wait_ge(zeroed, 1)
            sp.dma_start(xn2[NTOK:NTOK + P, :], zero_rows[:]).then_inc(blank, 16)
            sp.dma_start(out[NTOK:NTOK + P, :], zero_rows[:]).then_inc(blank, 16)
            for e in range(SLOTS):
                load_weights(sp, e, e, gate_up_w, down_w, w1, w2, w_loaded)
            sp.wait_ge(blank, 32)

        @block.gpsimd
        def _(pool):
            nc.gpsimd.memset(zero_rows[:], 0.0).then_inc(zeroed, 1)
            nc.gpsimd.memset(ones[:], 1.0).then_inc(zeroed, 1)
            pool.wait_ge(consts, 64)

            def weights_at_tiles(t, h, first, last):
                pool.wait_ge(is_tile_ready, t + 1)
                if not first:
                    pool.wait_ge(listed, 2 * TT * (t - 1))
                value_at_tile(nc.gpsimd, t, h, 1, weight).then_inc(weight_ready, 1)
            turns(pool, weights_at_tiles)

        @block.scalar
        def _(act):
            act.wait_ge(shifted, 1)
            nc.scalar.activation(p[:], p[:], ACT.Exp).then_inc(exp_done, 1)

        @block.tensor
        def _(pe):
            pe.wait_ge(consts, 64)
            pe.wait_ge(counted, 1)
            for k in range(2):
                last = nc.tensor.matmul(ps[:, k, 0:NT * E], lower[:, k, :], both[:].rearrange("p t e -> p (t e)"),
                                        start=True, stop=True)
            last.then_inc(counted, 1)

            def collect(t, h, first, last):
                pe.wait_ge(row_ready, t + 1)
                pe.wait_ge(number_ready, t + 1)
                pe.wait_ge(weight_ready, t + 1)
                for i in range(2 * TT):
                    nc.tensor.matmul(ps[:, 2, 0:2 * TILES], is_row[:, h, i, :],
                                     at_tile[:, h, i, :, :].rearrange("p a t -> p (a t)"),
                                     start=first and h == 0 and i == 0,
                                     stop=last and h == 1 and i == 2 * TT - 1).then_inc(listed, 1)
            turns(pe, collect)

        @block.vector
        def _(dve):
            v = nc.vector
            n = [0]

            def then(ins):
                n[0] += 1
                ins.then_inc(step, 1)
                dve.wait_ge(step, n[0])

            dve.wait_ge(consts, 64)
            dve.wait_ge(zeroed, 2)
            then(v.reduce_max(row["m"][:], logits[:], AXX))
            v.tensor_tensor(p[:], logits[:], over_e(row["m"]), ALU.subtract).then_inc(shifted, 1)
            dve.wait_ge(exp_done, 1)
            then(v.reduce_sum(row["s"][:], p[:], AXX))
            then(v.reciprocal(row["r"][:], row["s"][:]))
            then(v.tensor_tensor(p[:], p[:], over_e(row["r"]), ALU.mult))

            def choose(src, m, i, one):
                then(v.reduce_max(row[m][:], src[:], AXX))
                then(v.tensor_tensor(cand[:], src[:], over_e(row[m]), ALU.is_equal))
                then(v.scalar_tensor_tensor(out=cand[:], in0=cand[:], scalar=-float(E), in1=over_t(expert[:, 1, :]),
                                            op0=ALU.mult, op1=ALU.add))
                then(v.tensor_reduce(row[i][:], cand[:], AXX, ALU.min))
                then(v.tensor_tensor(one[:], over_t(expert[:, 0, :]), over_e(row[i]), ALU.is_equal))

            choose(p, "m1", "i1", one1)
            then(v.scalar_tensor_tensor(out=p2[:], in0=one1[:], scalar=-2.0, in1=p[:], op0=ALU.mult, op1=ALU.add))
            choose(p2, "m2", "i2", one2)
            v.tensor_tensor(both[:], one1[:], one2[:], ALU.add).then_inc(counted, 1)
            then(v.tensor_tensor(row["den"][:], row["m1"][:], row["m2"][:], ALU.add))
            then(v.reciprocal(row["den"][:], row["den"][:]))
            then(v.tensor_tensor(weight[:, :, 0], row["m1"][:], row["den"][:], ALU.mult))
            then(v.tensor_tensor(weight[:, :, 1], row["m2"][:], row["den"][:], ALU.mult))
            dve.wait_ge(counted, 2)
            tot = ps[:, 1, 0:NT * E].rearrange("p (t e) -> p t e", e=E)
            for e in range(E):
                then(v.tensor_tensor_scan(upto[:, :, e], ones[:], tot[:, :, e], 0.0, ALU.mult, ALU.add))
            then(v.tensor_tensor(where[:], upto[:], tot, ALU.subtract))
            then(v.tensor_tensor(where[:], ps[:, 0, 0:NT * E].rearrange("p (t e) -> p t e", e=E), where[:], ALU.add))
            then(v.tensor_scalar(nt_f[:], upto[:, NT - 1, :], float(P - 1), None, ALU.add))
            then(v.tensor_copy(nt_i[:], nt_f[:]))
            then(v.tensor_scalar(nt_i[:], nt_i[:], 7, None, ALU.arith_shift_right))
            then(v.tensor_copy(nt_f[:], nt_i[:]))
            then(v.tensor_tensor_scan(tend[:], ones[:, 0:E], nt_f[:], 0.0, ALU.mult, ALU.add))
            then(v.tensor_tensor(tstart[:], tend[:], nt_f[:], ALU.subtract))
            then(v.tensor_scalar(tstart[:], tstart[:], float(P), None, ALU.mult))
            then(v.tensor_tensor(where[:], where[:], over_t(tstart[:]), ALU.add))
            for k, one in enumerate((one1, one2)):
                then(v.tensor_tensor(cand[:], one[:], where[:], ALU.mult))
                then(v.reduce_sum(pos[:, :, k], cand[:], AXX))
            then(v.tensor_copy(pos_i[:], pos[:]))
            then(v.tensor_scalar(low_i[:], pos_i[:], P - 1, None, ALU.bitwise_and))
            then(v.tensor_scalar(pos_i[:], pos_i[:], 7, None, ALU.arith_shift_right))
            then(v.tensor_copy(tile_of[:], pos_i[:]))
            then(v.tensor_copy(row_of[:], low_i[:]))
            v.tensor_tensor(number[:], token[:, 0:NT].unsqueeze(2).to_broadcast([P, NT, 2]), row_of[:],
                            ALU.subtract).then_inc(placed, 1)
            dve.wait_ge(placed, 1)

            def ones_and_numbers(t, h, first, last):
                if not first:
                    dve.wait_ge(listed, 2 * TT * (t - 1))
                for ones_at, of, width, ready in ((is_tile, tile_of, TILES, is_tile_ready), (is_row, row_of, P, row_ready)):
                    wide = [P, 2 * TT, width]
                    v.tensor_tensor(ones_at[:, h], iota[:, 0:width].unsqueeze(1).to_broadcast(wide),
                                    of_turn(of, t).unsqueeze(2).to_broadcast(wide), ALU.is_equal).then_inc(ready, 1)
                dve.wait_ge(is_tile_ready, t + 1)
                value_at_tile(v, t, h, 0, number).then_inc(number_ready, 1)
            turns(dve, ones_and_numbers)
            then(v.tensor_tensor(passed[:], iota[0:1, 0:TILES].unsqueeze(2).to_broadcast([1, TILES, E]),
                                 tend[0:1, :].unsqueeze(1).to_broadcast([1, TILES, E]), ALU.is_ge))
            then(v.reduce_sum(eid[:], passed[:], AXX))
            then(v.tensor_scalar(eid[:], eid[:], float(E - 1), None, ALU.min))
            then(v.tensor_copy(expert_i[:], eid[:]))
            then(v.tensor_scalar(tables[:, 0, :], expert_i[:], SLOTS - 1, None, ALU.bitwise_and))
            then(v.tensor_scalar(need[:], eid[:], float(LOADS), float(LOADS), ALU.mult, ALU.add))
            then(v.tensor_copy(tables[:, 1, :], need[:]))
            then(v.tensor_scalar(need[:, 0:E], tend[0:1, :], 1.0, None, ALU.add))
            then(v.tensor_copy(tables[:, 2, 0:E], need[:, 0:E]))
            dve.wait_ge(listed, 2 * NT)
            then(v.tensor_scalar(ids[:], ps[:, 2, 0:TILES], token[:, NT:NT + 1], None, ALU.add))
            then(v.tensor_copy(weights[:], ps[:, 2, TILES:2 * TILES]))


def load_weights(sp, e, s, gate_up_w, down_w, w1, w2, w_loaded):
    if e:
        sp.wait_ge(w_loaded, LOADS * e)
    for c in range(w1.shape[2]):
        sp.dma_start(w1[:, s, c, :], gate_up_w[e, c * P:(c + 1) * P, :]).then_inc(w_loaded, 16)
    sp.dma_start(w2[:, s, :, :], down_w[e].rearrange("(c p) d -> p c d", p=P)).then_inc(w_loaded, 16)


def experts_phase(nc, xn2, tables, ids, weights, gate_up_w, down_w, w1, w2, w_loaded, ident_c, out):
    E, D, F2 = gate_up_w.shape
    F = F2 // 2
    TILES = tables.shape[2]
    KD, KF = D // P, F // P
    NROWS = out.shape[0]
    U = 4

    with ExitStack() as ctx:
        def sb(name, shape, dt=F32):
            return ctx.enter_context(nc.sbuf_tensor(name, shape, dt))

        def sem(name):
            return ctx.enter_context(nc.semaphore(name))

        ident = sb("e_ident", [P, P])
        xg = sb("e_xg", [P, U, D])
        who = sb("e_who", [P, U], U32)
        xT = sb("e_xT", [P, 2, KD, P])
        gact = sb("e_gact", [P, 2, BANK])
        hact = sb("e_hact", [P, 2, F])
        hT = sb("e_hT", [P, 2, KF, P])
        y = sb("e_y", [P, 2, D])
        ps = ctx.enter_context(nc.psum_tensor("e_ps", [P, 8, BANK], F32))
        T_BANK, Y_BANK, X_BANK = 4, 6, 7

        consts = sem("e_consts")
        who_ready = sem("e_who_ready")
        x_loaded = [sem(f"e_x_loaded{i}") for i in range(U)]
        x_turned, xT_ready = sem("e_x_turned"), sem("e_xT_ready")
        gu_done, g_ready, h_ready = sem("e_gu_done"), sem("e_g_ready"), sem("e_h_ready")
        h_turned, hT_ready = sem("e_h_turned"), sem("e_hT_ready")
        y_done, y_ready, added = sem("e_y_done"), sem("e_y_ready"), sem("e_added")
        held = sem("e_held")

        def hold(eng, of, value):
            eng.wait_ge(of, value)
            eng.sem_inc(held, 1)

        def groups(eng, body):
            n = TILES // U
            for j in range(U):
                body(j, 0, j, j == 0, False)
            with eng.Fori(1, n - 1) as g:
                for j in range(U):
                    body(U * g + j, g, j, False, False)
            for j in range(U):
                i = TILES - U + j
                body(i, n - 1, j, False, i + 1 == TILES)

        block = ctx.enter_context(nc.Block())

        ONE = 1

        @block.sync
        def _(sp):
            sp.sem_inc(y_done, ONE)
            for e in range(SLOTS, E):
                end = sp.value_load(tables[0:1, 2, e - SLOTS:e - SLOTS + 1], min_val=1, max_val=TILES + 1)
                sp.wait_ge(y_done, end)
                load_weights(sp, e, e % SLOTS, gate_up_w, down_w, w1, w2, w_loaded)
            sp.wait_ge(added, 16 * TILES)

        @block.gpsimd
        def _(pool):
            nc.gpsimd.dma_start(ident[:], ident_c).then_inc(consts, 16)

            def load(i, j):
                nc.gpsimd.tensor_copy(who[:, j % U:j % U + 1], ids[:, bass.ds(i, 1)]).then_inc(who_ready, 1)
                hold(pool, who_ready, i + 1)
                nc.gpsimd.indirect_dma_start(
                    out=xg[:, j % U, :], out_offset=None, in_=xn2,
                    in_offset=bass.IndirectOffsetOnAxis(ap=who[:, j % U:j % U + 1], axis=0)).then_inc(x_loaded[j % U], 16)

            for j in range(U - 1):
                load(j, j)

            def tile(i, g, j, first, last):
                if not first:
                    hold(pool, added, 16 * i)
                if not isinstance(i, int) or i + U - 1 < TILES:
                    load(i + U - 1, j + U - 1)
                hold(pool, y_ready, i + 1)
                nc.gpsimd.indirect_dma_start(
                    out=out, out_offset=bass.IndirectOffsetOnAxis(ap=who[:, j:j + 1], axis=0),
                    in_=y[:, j % 2, :], in_offset=None, compute_op=ALU.add).then_inc(added, 16)
            groups(pool, tile)

        @block.scalar
        def _(act):
            def turn_x(i, j):
                act.wait_ge(x_turned, i + 1)
                nc.scalar.activation(xT[:, j % 2, :, :].rearrange("p c t -> p (c t)"), ps[:, X_BANK, 0:D],
                                     ACT.Copy).then_inc(xT_ready, 1)

            def gelu(i, h):
                act.wait_ge(gu_done, 2 * i + h + 1)
                nc.scalar.activation(gact[:, h, :], ps[:, 2 * h, :], ACT.Gelu).then_inc(g_ready, 1)

            def turn_h(i, j, h):
                act.wait_ge(h_turned, 2 * i + h + 1)
                nc.scalar.activation(hT[:, j % 2, h * KF // 2:(h + 1) * KF // 2, :].rearrange("p c t -> p (c t)"),
                                     ps[:, T_BANK + h, :], ACT.Copy).then_inc(hT_ready, 1)

            turn_x(0, 0)

            def tile(i, g, j, first, last):
                if not first:
                    act.wait_ge(h_ready, 2 * i)
                gelu(i, 0)
                if not first:
                    turn_h(i - 1, j - 1, 1)
                gelu(i, 1)
                if not last:
                    turn_x(i + 1, j + 1)
                if not (isinstance(i, int) and i < 2):
                    act.wait_ge(y_done, ONE + i - 1)
                turn_h(i, j, 0)
            groups(act, tile)
            turn_h(TILES - 1, U - 1, 1)

        @block.vector
        def _(dve):
            def weigh(i, j):
                dve.wait_ge(y_done, ONE + i + 1)
                if not (isinstance(i, int) and i < 2):
                    dve.wait_ge(added, 16 * (i - 1))
                nc.vector.tensor_scalar(y[:, j % 2, :], ps[:, Y_BANK, 0:D], weights[:, bass.ds(i, 1)], None,
                                        ALU.mult).then_inc(y_ready, 1)

            def tile(i, g, j, first, last):
                for h in range(2):
                    dve.wait_ge(g_ready, 2 * i + h + 1)
                    if not (isinstance(i, int) and i < 2):
                        dve.wait_ge(h_turned, 2 * (i - 1))
                    nc.vector.tensor_tensor(hact[:, j % 2, h * BANK:(h + 1) * BANK], gact[:, h, :],
                                            ps[:, 2 * h + 1, :], ALU.mult).then_inc(h_ready, 1)
                if not first:
                    weigh(i - 1, j - 1)

            groups(dve, tile)
            weigh(TILES - 1, U - 1)

        @block.tensor
        def _(pe):
            t = nc.tensor
            pe.wait_ge(consts, 16)

            def turn_x(i, j, g):
                pe.wait_ge(x_loaded[j % U], 16 * g + 16)
                if not (isinstance(i, int) and i == 0):
                    pe.wait_ge(xT_ready, i)
                for c in range(KD):
                    last = t.transpose(ps[:, X_BANK, c * P:(c + 1) * P], xg[:, j % U, c * P:(c + 1) * P], ident[:])
                last.then_inc(x_turned, 1)

            def gate_up(i, j, h, slot):
                if not (isinstance(i, int) and i == 0):
                    pe.wait_ge(h_ready, 2 * i + h - 1)
                for which in range(2):
                    lo = which * F + h * BANK
                    for c in range(KD):
                        last = t.matmul(ps[:, 2 * h + which, :], xT[:, j % 2, c, :],
                                        w1[:, bass.ds(slot, 1), c, lo:lo + BANK].rearrange("p a n -> p (a n)"),
                                        start=(c == 0), stop=(c == KD - 1))
                last.then_inc(gu_done, 1)

            def turn_h(i, j, h):
                pe.wait_ge(h_ready, 2 * i + h + 1)
                if not (isinstance(i, int) and i == 0):
                    pe.wait_ge(hT_ready, 2 * i + h - 1)
                for c in range(KF // 2):
                    lo = h * BANK + c * P
                    last = t.transpose(ps[:, T_BANK + h, c * P:(c + 1) * P], hact[:, j % 2, lo:lo + P], ident[:])
                last.then_inc(h_turned, 1)

            def down(i, j, slot):
                pe.wait_ge(hT_ready, 2 * i + 2)
                if not (isinstance(i, int) and i == 0):
                    pe.wait_ge(y_ready, i)
                for c in range(KF):
                    last = t.matmul(ps[:, Y_BANK, 0:D], hT[:, j % 2, c, :],
                                    w2[:, bass.ds(slot, 1), c, :].rearrange("p a n -> p (a n)"),
                                    start=(c == 0), stop=(c == KF - 1))
                last.then_inc(y_done, 1)

            def entry(k, i, most):
                return pe.value_load(tables[0:1, k, bass.ds(i, 1)], min_val=0, max_val=most)

            turn_x(0, 0, 0)

            def tile(i, g, j, first, last):
                slot = entry(0, i, SLOTS - 1)
                pe.wait_ge(w_loaded, pe.value_load(tables[0:1, 1, bass.ds(i, 1)], min_val=LOADS, max_val=LOADS * E))
                pe.wait_ge(xT_ready, i + 1)
                gate_up(i, j, 0, slot)
                if not first:
                    turn_h(i - 1, j - 1, 1)
                gate_up(i, j, 1, slot)
                if not last:
                    turn_x(i + 1, j + 1, g + (j + 1) // U)
                if not first:
                    down(i - 1, j - 1, entry(0, i - 1, SLOTS - 1))
                turn_h(i, j, 0)
            groups(pe, tile)
            turn_h(TILES - 1, U - 1, 1)
            down(TILES - 1, U - 1, entry(0, TILES - 1, SLOTS - 1))


def decoder_layer(nc, a, out):
    NB, T, DM = a["x"].shape
    N = a["a_log"].shape[1]
    NTOK = NB * T
    E, F2 = a["gate_up_w"].shape[0], a["gate_up_w"].shape[2]
    NT = NTOK // P
    TILES = 2 * NT + E
    c_rows = nc.dram_tensor("c_rows", (NB, N, T), F32).ap()
    x1 = nc.dram_tensor("x1", (NB, T, DM), F32).ap()
    xn2 = nc.dram_tensor("xn2", (NTOK + P, DM), F32).ap()
    x2 = out[0:NTOK, :].rearrange("(b t) d -> b t d", b=NB)
    mamba_phase(nc, a["x"], a["in_w"], a["conv_w"], a["xproj_w"], a["dtproj_w"], a["dtproj_b"], a["a_log"],
                a["d_vec"], a["out_w"], a["ident"], a["sel"], c_rows, x1)
    with nc.sbuf_tensor("logits", [P, NT, E], F32) as logits:
        attention_phase(nc, x1, a["ctx_t"], a["pos"], a["wq"], a["wk"], a["wv"], a["wo"], a["bq"], a["bk"],
                        a["bv"], a["bo"], a["ident"], a["head_mask"], a["v_mask"], a["inv_freq"], a["gate_w"],
                        x2, xn2[0:NTOK, :], logits)
        with nc.sbuf_tensor("tables", [1, 3, TILES], I32) as tables, nc.sbuf_tensor("ids", [P, TILES], U32) as ids, \
             nc.sbuf_tensor("weights", [P, TILES], F32) as weights, nc.semaphore("w_loaded") as w_loaded, \
             nc.sbuf_tensor("w1", [P, SLOTS, DM // P, F2], F32) as w1, \
             nc.sbuf_tensor("w2", [P, SLOTS, F2 // 2 // P, DM], F32) as w2:
            dispatch_phase(nc, logits, a["lower"], a["token"], a["expert"], a["iota"], a["gate_up_w"], a["down_w"],
                           w1, w2, w_loaded, tables, ids, weights, xn2, out)
            experts_phase(nc, xn2, tables, ids, weights, a["gate_up_w"], a["down_w"], w1, w2, w_loaded,
                          a["ident"], out)


def kernel(**inputs):
    import concourse.bacc as bacc
    from concourse.bass_utils import run_bass_kernel_spmd

    i = {k: np.asarray(v) for k, v in inputs.items()}
    B, T, D = i["x"].shape
    ED, _, KC = i["L0_attn_conv_w"].shape
    N = i["L0_attn_A_log"].shape[1]
    E = i["L0_ffn_gate_w"].shape[0]
    HD = 16
    NTOK = B * T
    NT = NTOK // P
    f32 = np.float32
    sel = np.zeros((3 * N, N, P), f32)
    for n in range(N):
        sel[n::N, n] = 1
    inv_freq = (f32(1) / f32(10000) ** (np.arange(0, HD, 2, dtype=f32) / f32(HD))).astype(f32)
    e = np.arange(E)
    M = i["ctx_1024"].shape[1]
    G = -(-(P // HD) * M // P)
    v_rows = (np.arange(G) * P + np.arange(P)[:, None]) // M
    arrays = dict(
        x=i["x"], in_w=i["L0_attn_in_proj_w"].T, conv_w=i["L0_attn_conv_w"][:, 0, :], xproj_w=i["L0_attn_x_proj_w"].T,
        dtproj_w=i["L0_attn_dt_proj_w"].T, dtproj_b=i["L0_attn_dt_proj_b"].reshape(ED // P, P).T,
        a_log=i["L0_attn_A_log"], d_vec=i["L0_attn_D"].reshape(ED // P, P).T, out_w=i["L0_attn_out_proj_w"].T,
        ident=np.eye(P, dtype=f32), sel=sel.reshape(3 * N, N * P),
        ctx_t=i["ctx_1024"].reshape(-1, D).T, pos=i["itok_BxS_1_4095"].reshape(NT, P).T,
        wq=i["L0_xattn_Wq"].T, wk=i["L0_xattn_Wk"].T, wv=i["L0_xattn_Wv"].T, wo=i["L0_xattn_Wo"].T,
        bq=i["L0_xattn_bq"], bk=i["L0_xattn_bk"].reshape(D // P, P).T, bv=i["L0_xattn_bv"], bo=i["L0_xattn_bo"],
        head_mask=(np.arange(P)[:, None] // HD == np.arange(P // HD)).astype(f32),
        v_mask=(v_rows[:, :, None] == np.arange(P // HD)).astype(f32),
        inv_freq=np.tile(inv_freq, (P, 1)), gate_w=i["L0_ffn_gate_w"].T,
        lower=np.stack([np.triu(np.ones((P, P), f32), 1), np.ones((P, P), f32)], 1),
        token=(np.append(np.arange(NT) * P - NTOK, NTOK) + np.arange(P)[:, None]).astype(f32),
        expert=np.tile(np.stack([e, e + E]).astype(f32), (P, 1, 1)), iota=np.tile(np.arange(P, dtype=f32), (P, 1)),
        gate_up_w=i["L0_ffn_gate_up_w"].transpose(0, 2, 1), down_w=i["L0_ffn_down_w"].transpose(0, 2, 1),
    )
    arrays = {k: np.ascontiguousarray(v) for k, v in arrays.items()}
    nc = bacc.Bacc("TRN2", target_bir_lowering=False, num_devices=1)
    aps = {k: nc.dram_tensor(f"in_{k}", v.shape, mybir.dt.from_np(v.dtype), kind="ExternalInput").ap()
           for k, v in arrays.items()}
    out = nc.dram_tensor("out_0", (NTOK + P, D), F32, kind="ExternalOutput").ap()
    decoder_layer(nc, aps, out)
    r = run_bass_kernel_spmd(nc, [{f"in_{k}": v for k, v in arrays.items()}], core_ids=[0])
    return r.results[0]["out_0"][0:NTOK].reshape(B, T, D)
```
